# Optimizing a Trainium2 kernel written in Bass

```python
import numpy as np
import jax
import jax.numpy as jnp

def _softmax(x, axis=-1):
    return jax.nn.softmax(x, axis=axis)

def _gelu(x):
    return jax.nn.gelu(x, approximate=True)

def _silu(x):
    return jax.nn.silu(x)

def _sigmoid(x):
    return jax.nn.sigmoid(x)

def _layernorm(x, axis=-1, eps=1e-05):
    m = jnp.mean(x, axis=axis, keepdims=True)
    v = jnp.var(x, axis=axis, keepdims=True)
    return (x - m) / jnp.sqrt(v + eps)

def _scatter_add(tgt, idx, src, axis=0):
    return tgt.at[idx].add(src)

def _segment_sum(src, seg, n):
    return jax.ops.segment_sum(src, seg, n)
kernel_name = 'mk_xattn_ffn_d1_seqx_r8_2b48e6'

def setup_inputs(seed: int=0):
    np.random.seed(seed)
    _w = jnp.asarray

    def _rec_inputs():
        import jax
        import jax.numpy as jnp
        _rk = jax.random.key(seed)
        x = -0.000125 + 0.9999 * jax.random.normal(jax.random.fold_in(_rk, 1), (4, 256, 256), jnp.float32)
        _lenS = 256 - jax.random.randint(jax.random.fold_in(_rk, 7), (4,), 0, max(1, 256 // 4) + 1, jnp.int32)
        _lenS2 = 256 - jax.random.randint(jax.random.fold_in(_rk, 8), (4,), 0, max(1, 256 // 4) + 1, jnp.int32)
        itok_BxS_13_99985 = jax.random.randint(jax.random.fold_in(_rk, 11), (4, 256), 13, 99986, jnp.int32)
        _ctx_2048P = jax.random.normal(jax.random.fold_in(_rk, 12), (4, 16, 256), jnp.float32)
        _ctx_2048c = jax.random.dirichlet(jax.random.fold_in(_rk, 512), 0.3 * jnp.ones((16,), jnp.float32), (4, 256))
        _ctx_2048t = jnp.einsum('bsk,bkd->bsd', _ctx_2048c, _ctx_2048P)
        _ctx_2048t = _ctx_2048t * jax.lax.rsqrt(jnp.mean(jnp.square(_ctx_2048t)) + 1e-12) * 0.953939
        ctx_2048 = 6.82029e-06 + 0.0200006 * (_ctx_2048t + 0.3 * jax.random.normal(jax.random.fold_in(_rk, 612), (4, 256, 256), jnp.float32))
        return (x, itok_BxS_13_99985, ctx_2048)
    x, itok_BxS_13_99985, ctx_2048 = _rec_inputs()

    def _L0_xattn_setup():
        import jax, jax.numpy as jnp
        import numpy as np
        B, S, D = (4, 512, 256)
        E = 4
        F = 1024 // E
        VOCAB = 12500
        key = jax.random.key(seed)
        k1, k2, k3, k4, k5 = jax.random.split(key, 5)
        hidden_states = jax.random.normal(k1, (B, S, D), dtype=jnp.float32)
        token_ids = jax.random.randint(k2, (B, S), 0, VOCAB, dtype=jnp.int64)
        Wg = jax.random.normal(k3, (E, F, D), dtype=jnp.float32) * 0.02
        Wu = jax.random.normal(k4, (E, F, D), dtype=jnp.float32) * 0.02
        Wd = jax.random.normal(k5, (E, D, F), dtype=jnp.float32) * 0.02
        return {'hidden_states': hidden_states, 'token_ids': token_ids, 'Wg': Wg, 'Wu': Wu, 'Wd': Wd}
    _L0_xattn_all = _L0_xattn_setup()
    _L0_xattn_in = {k: v for k, v in _L0_xattn_all.items() if k in ()}
    del _L0_xattn_all

    def _L0_ffn_setup():
        import jax, jax.numpy as jnp
        import numpy as np
        B, T, C = (2, 128, 256)
        E, TOPK = (8, 2)
        F_MOE = 176
        F_SHARED = 704
        key = jax.random.key(seed)
        ks = jax.random.split(key, 9)
        s = 0.02
        return {'x': jax.random.normal(ks[0], (B, T, C), dtype=jnp.float32), 'gate_w': jax.random.normal(ks[1], (E, C), dtype=jnp.float32) * s, 'expert_fc1': jax.random.normal(ks[2], (E, F_MOE, C), dtype=jnp.float32) * s, 'expert_fc2': jax.random.normal(ks[3], (E, F_MOE, C), dtype=jnp.float32) * s, 'expert_proj': jax.random.normal(ks[4], (E, C, F_MOE), dtype=jnp.float32) * s, 'shared_fc1': jax.random.normal(ks[5], (F_SHARED, C), dtype=jnp.float32) * s, 'shared_fc2': jax.random.normal(ks[6], (F_SHARED, C), dtype=jnp.float32) * s, 'shared_proj': jax.random.normal(ks[7], (C, F_SHARED), dtype=jnp.float32) * s, 'shared_gate_w': jax.random.normal(ks[8], (1, C), dtype=jnp.float32) * s}
    _L0_ffn_all = _L0_ffn_setup()
    _L0_ffn_in = {k: v for k, v in _L0_ffn_all.items() if k in ('gate_w', 'expert_fc1', 'expert_fc2', 'expert_proj', 'shared_fc1', 'shared_fc2', 'shared_proj', 'shared_gate_w')}
    del _L0_ffn_all
    return {'x': x, 'itok_BxS_13_99985': itok_BxS_13_99985, 'ctx_2048': ctx_2048, 'L0_ffn_gate_w': _L0_ffn_in['gate_w'], 'L0_ffn_expert_fc1': _L0_ffn_in['expert_fc1'], 'L0_ffn_expert_fc2': _L0_ffn_in['expert_fc2'], 'L0_ffn_expert_proj': _L0_ffn_in['expert_proj'], 'L0_ffn_shared_fc1': _L0_ffn_in['shared_fc1'], 'L0_ffn_shared_fc2': _L0_ffn_in['shared_fc2'], 'L0_ffn_shared_proj': _L0_ffn_in['shared_proj'], 'L0_ffn_shared_gate_w': _L0_ffn_in['shared_gate_w']}

def reference(x, itok_BxS_13_99985, ctx_2048, L0_ffn_gate_w, L0_ffn_expert_fc1, L0_ffn_expert_fc2, L0_ffn_expert_proj, L0_ffn_shared_fc1, L0_ffn_shared_fc2, L0_ffn_shared_proj, L0_ffn_shared_gate_w):
    import jax
    import jax.numpy as jnp

    def _L0_xattn_ref(hidden_states, token_ids, Wg, Wu, Wd):
        import jax, jax.numpy as jnp
        import numpy as np
        B, S, D = (4, 512, 256)
        E = 4
        F = 1024 // E
        VOCAB = 12500
        tokens_per_expert = VOCAB // E
        tid = jnp.clip(token_ids, 0, VOCAB - 1)
        expert_ids = jnp.minimum(tid // tokens_per_expert, E - 1)
        out = jnp.zeros_like(hidden_states)
        for e in range(E):
            g = jax.nn.silu(jnp.einsum('bsd,fd->bsf', hidden_states, Wg[e]))
            u = jnp.einsum('bsd,fd->bsf', hidden_states, Wu[e])
            y = jnp.einsum('bsf,df->bsd', g * u, Wd[e])
            out = jnp.where((expert_ids == e)[..., None], y, out)
        return out

    def _L0_ffn_ref(x, gate_w, expert_fc1, expert_fc2, expert_proj, shared_fc1, shared_fc2, shared_proj, shared_gate_w):
        import jax, jax.numpy as jnp
        import numpy as np
        B, T, C = (2, 128, 256)
        E, TOPK = (8, 2)
        F_MOE = 176
        F_SHARED = 704
        b, t, c = x.shape
        xf = x.reshape(-1, c)
        n = xf.shape[0]
        router = xf @ gate_w.T
        probs = jax.nn.softmax(router.astype(jnp.float32), axis=1).astype(x.dtype)
        top_p, top_i = jax.lax.top_k(probs, TOPK)
        combine = jnp.zeros((n, E), dtype=x.dtype).at[jnp.arange(n)[:, None], top_i].set(top_p)
        h1 = jnp.einsum('nc,efc->enf', xf, expert_fc1)
        h2 = jnp.einsum('nc,efc->enf', xf, expert_fc2)
        h = jax.nn.silu(h1) * h2
        out_e = jnp.einsum('enf,ecf->enc', h, expert_proj)
        y = jnp.einsum('ne,enc->nc', combine, out_e)
        s1 = xf @ shared_fc1.T
        s2 = xf @ shared_fc2.T
        shared = jax.nn.silu(s1) * s2 @ shared_proj.T
        y = y + jax.nn.sigmoid(xf @ shared_gate_w.T) * shared
        return y.reshape(b, t, c)
    x = x + _L0_xattn_ref(_layernorm(x, axis=-1), itok_BxS_13_99985, ctx_2048, ctx_2048, ctx_2048)
    x = x + _L0_ffn_ref(_layernorm(x, axis=-1), L0_ffn_gate_w, L0_ffn_expert_fc1, L0_ffn_expert_fc2, L0_ffn_expert_proj, L0_ffn_shared_fc1, L0_ffn_shared_fc2, L0_ffn_shared_proj, L0_ffn_shared_gate_w)
    return x

_drawn_inputs = setup_inputs


def setup_inputs(seed=0):
    import zlib

    import numpy as np

    out = dict(_drawn_inputs(seed))
    spreads = {}
    factors = {'L0_ffn_gate_w': 8.0,
     'L0_ffn_expert_fc1': 8.0,
     'L0_ffn_expert_fc2': 8.0,
     'L0_ffn_expert_proj': 8.0,
     'L0_ffn_shared_fc1': 3.984,
     'L0_ffn_shared_fc2': 3.964,
     'L0_ffn_shared_proj': 3.954,
     'L0_ffn_shared_gate_w': 8.0}
    for name, (base, spread) in spreads.items():
        noise = np.random.default_rng([zlib.crc32(name.encode()), seed]).standard_normal(out[name].shape)
        drawn = base * np.exp(spread * noise) if base else spread * noise
        out[name] = jnp.asarray(drawn.astype(out[name].dtype))
    for name, factor in factors.items():
        out[name] = (out[name] * factor).astype(out[name].dtype)
    return out
```

```python
from contextlib import ExitStack

import concourse.bass as bass
from concourse import mybir

ALU = mybir.AluOpType
ACT = mybir.ActivationFunctionType
AX = mybir.AxisListType
F32 = mybir.dt.float32
F32R = mybir.dt.float32r
BF16 = mybir.dt.bfloat16
I32 = mybir.dt.int32
U32 = mybir.dt.uint32

P = 128
D = 256
KD = D // P
TOK = 1024
NT = TOK // P
HALF = 512
TH = HALF // P
E1 = 4
F1 = 256
VOCAB = 12500
E2 = 8
F2 = 176
FS = 704
NJ1 = E1 * F1 // P
NJX = E2 * F2 // P
NJS = -(-FS // P)
NJ2 = NJX + NJS
WT = 3 * D
GW = 16
NG = 10
EPS = 1e-5
LAG = 2
NSTAGE = 3


def schedule():
    h1 = [("u1", 0, j) for j in range(NJ1)], [("u1", 1, j) for j in range(NJ1)]
    sh = [("us", 0, j) for j in range(NJS)], [("us", 1, j) for j in range(NJS)]
    ex = [("ux", 0, j) for j in range(NJX)], [("ux", 1, j) for j in range(NJX)]
    return ([("t", 0, 0), ("t", 1, 0)] + h1[0] + h1[1][:6] + [("t", 0, 0)] + h1[1][6:]
            + sh[0][:5] + [("t", 1, 0), ("r", 0, 0)] + sh[0][5:] + sh[1][:4] + [("c", 0, 0)] + sh[1][4:]
            + ex[0] + ex[1])


STEPS = schedule()
UNITS = [i for i, s in enumerate(STEPS) if s[0][0] == "u"]
T_STEPS = [i for i, s in enumerate(STEPS) if s[0] == "t"]
LAST_OF_GROUP = {"u1": NJ1 - 1, "us": NJS - 1, "ux": NJX - 1}


def downs_after(i):
    n = len(STEPS)
    if i < n - 1:
        return [u for u, s in enumerate(UNITS) if s + LAG == i]
    return [u for u, s in enumerate(UNITS) if s + LAG >= i]


def ends_group(u):
    kind, _, j = STEPS[UNITS[u]]
    return j == LAST_OF_GROUP[kind]


def group_of(u):
    return sum(ends_group(v) for v in range(u))


def first_of_group(u):
    return STEPS[UNITS[u]][2] == 0


def units_until(i):
    return sum(s < i for s in UNITS)


def t_index(i):
    return sum(s[0] == "t" for s in STEPS[:i])


def program(nc, x, ids, ctx_t, w2, gate, out):
    with ExitStack() as ctx:
        def sb(name, shape, dt):
            return ctx.enter_context(nc.sbuf_tensor(name, shape, dt))

        def sem(name):
            return ctx.enter_context(nc.semaphore(name))

        w1_hi = sb("w1_hi", [P, E1, KD, F1], F32R)
        w1_lo = sb("w1_lo", [P, E1, KD, F1], F32R)
        w2_hi = sb("w2_hi", [P, NJ2, WT], F32R)
        w2_lo = sb("w2_lo", [P, NJ2, WT], F32R)
        g_raw = sb("g_raw", [P, KD, NG], F32)
        g_hi = sb("g_hi", [P, KD, NG], F32R)
        g_lo = sb("g_lo", [P, KD, NG], F32R)
        stage = sb("stage", [P, NSTAGE, WT], F32)
        xs = sb("xs", [P, NT, D], F32)
        xn = sb("xn", [P, TH, D], F32)
        xt_hi = sb("xt_hi", [P, KD, TOK], F32R)
        xt_lo = sb("xt_lo", [P, KD, TOK], F32R)
        idb = sb("idb", [P, HALF], I32)
        eid = sb("eid", [P, HALF], BF16)
        mask = sb("mask", [P, E1, TOK], BF16)
        work = sb("work", [P, 6, HALF], F32)
        sg = work[:, 0:2]
        sm = work[:, 2:4]
        hf = work[:, 4:6]
        h_hi = sb("h_hi", [P, 3, HALF], F32R)
        h_lo = sb("h_lo", [P, 3, HALF], F32R)
        ident = sb("ident", [P, P], F32)
        iota8 = sb("iota8", [P, E2], F32)
        sel_f = work[0:E2].rearrange("e a b -> e (a b)")[:, 0:NJX * P]
        sel = sb("sel", [E2, NJX * P], F32R)
        half_neg = sb("half_neg", [P, TH], F32)
        st = sb("st", [P, NT, 6], F32)
        mv = sb("mv", [P, NT, 2], F32)
        ve = sb("ve", [P, NT], F32)
        rstd = sb("rstd", [P, NT], F32)
        nmr = sb("nmr", [P, NT], F32)
        mx = sb("mx", [P, NT], F32)
        lg = sb("lg", [P, NT, E2], F32)
        ee = sb("ee", [P, NT, E2], F32)
        eg = sb("eg", [P, NT], F32)
        gs = sb("gs", [P, NT], F32)
        es = sb("es", [P, NT], F32)
        m8 = sb("m8", [P, NT, 8], F32)
        i8 = sb("i8", [P, NT, 8], U32)
        i8f = sb("i8f", [P, NT, 8], F32)
        comb = sb("comb", [P, NT, E2], F32)
        ct_hi = sb("ct_hi", [E2, TOK], F32R)
        ct_lo = sb("ct_lo", [E2, TOK], F32R)

        slot = [[ctx.enter_context(nc.psum_tensor(f"slot{i}_{b}", [P, HALF], F32)) for b in range(3)]
                for i in range(2)]
        yb = [ctx.enter_context(nc.psum_tensor(f"y{b}", [P, 2, D], F32)) for b in range(TH // 2)]

        x_in = [sem(f"x_in{h}") for h in range(2)]
        g_in = sem("g_in")
        ids_in = [sem(f"ids_in{h}") for h in range(2)]
        stage_in = [sem(f"stage_in{i}") for i in range(NSTAGE)]
        consts = sem("consts")
        sel_ok = sem("sel_ok")
        stage_free = sem("stage_free")
        whi_ok = sem("whi_ok")
        ghi_ok = sem("ghi_ok")
        g_ok = sem("g_ok")
        ids_used = sem("ids_used")
        mask_ok = sem("mask_ok")
        ve_ok = sem("ve_ok")
        rstd_ok = sem("rstd_ok")
        nmr_ok = sem("nmr_ok")
        xn_ok = sem("xn_ok")
        z_ok = sem("z_ok")
        drained = sem("drained")
        thi_ok = sem("thi_ok")
        silu_ok = sem("silu_ok")
        sm_ok = sem("sm_ok")
        hhi_ok = sem("hhi_ok")
        hlo_ok = sem("hlo_ok")
        down_ok = sem("down_ok")
        y_free = sem("y_free")
        lg_ok = sem("lg_ok")
        exp_ok = sem("exp_ok")
        comb_ok = sem("comb_ok")
        cthi_ok = sem("cthi_ok")
        chain = sem("chain")
        out_ok = sem("out_ok")
        stored = sem("stored")

        xf = x.rearrange("(t p) d -> p t d", p=P)
        of = out.rearrange("(t p) d -> p t d", p=P)
        NC1 = E1
        W2_ORDER = [NJX + j for j in range(NJS)] + list(range(NJX))
        NSTG = NC1 + NJ2

        def w2_ready(kind, j):
            tile = NJX + j if kind == "us" else j
            return NC1 + W2_ORDER.index(tile) + 1

        def stage_views(n):
            if n < NC1:
                raw = stage[:, n % NSTAGE, 0:KD * F1].rearrange("p (k f) -> p k f", k=KD)
                return raw, w1_hi[:, n], w1_lo[:, n]
            j = W2_ORDER[n - NC1]
            return stage[:, n % NSTAGE, 0:WT], w2_hi[:, j], w2_lo[:, j]

        block = ctx.enter_context(nc.Block())

        @block.sync
        def _(sp):
            for h in range(2):
                sp.dma_start(xs[:, TH * h:TH * h + TH], xf[:, TH * h:TH * h + TH]).then_inc(x_in[h], 16)
            for n in range(NSTG):
                if n >= NSTAGE:
                    sp.wait_ge(stage_free, n - NSTAGE + 1)
                if n < NC1:
                    src, dst = ctx_t[:, n], stage_views(n)[0]
                else:
                    src, dst = w2[W2_ORDER[n - NC1]], stage[:, n % NSTAGE, 0:WT]
                sp.dma_start(dst, src).then_inc(stage_in[n % NSTAGE], 16)
                if n == 1:
                    sp.dma_start(idb[:], ids[0:HALF].partition_broadcast(P)).then_inc(ids_in[0], 16)
                    sp.dma_start(g_raw[:], gate).then_inc(g_in, 16)
                if n == NSTAGE:
                    sp.wait_ge(ids_used, 1)
                    sp.dma_start(idb[:], ids[HALF:TOK].partition_broadcast(P)).then_inc(ids_in[1], 16)
            for t in range(NT):
                sp.wait_ge(out_ok, t + 1)
                sp.dma_start(of[:, t], xs[:, t]).then_inc(stored, 16)
            sp.wait_ge(stored, 16 * NT)

        @block.gpsimd
        def _(pool):
            nc.gpsimd.memset(half_neg[:], -0.5)
            nc.gpsimd.memset(ident[:], 0.0)
            nc.gpsimd.memset(sel_f, 1.0)
            nc.gpsimd.iota(iota8[:], pattern=[[1, E2]], base=0, channel_multiplier=0,
                           allow_small_or_imprecise_dtypes=True).then_inc(consts, 1)
            pool.wait_ge(consts, 1)
            nc.gpsimd.affine_select(out=ident[:], in_=ident[:], compare_op=ALU.not_equal, fill=1.0,
                                    base=0, pattern=[[-1, P]], channel_multiplier=1).then_inc(consts, 1)
            nc.gpsimd.affine_select(out=sel_f, in_=sel_f, compare_op=ALU.is_ge, fill=0.0, base=0,
                                    pattern=[[1, NJX * P]], channel_multiplier=-F2).then_inc(sel_ok, 1)
            pool.wait_ge(sel_ok, 1)
            nc.gpsimd.affine_select(out=sel_f, in_=sel_f, compare_op=ALU.is_gt, fill=0.0, base=F2,
                                    pattern=[[-1, NJX * P]], channel_multiplier=F2).then_inc(sel_ok, 1)
            pool.wait_ge(sel_ok, 2)
            nc.gpsimd.tensor_copy(sel[:], sel_f).then_inc(sel_ok, 1)

            def rstds(n):
                t = TH * (n % 2)
                pool.wait_ge(ve_ok, n + 1)
                nc.gpsimd.tensor_tensor(rstd[:, t:t + TH], ve[:, t:t + TH], half_neg[:],
                                        ALU.pow).then_inc(rstd_ok, 1)

            def split_lo(n):
                raw, hi, lo = stage_views(n)
                pool.wait_ge(whi_ok, n + 1)
                nc.gpsimd.tensor_tensor(lo, raw, hi.bitcast(F32), ALU.subtract).then_inc(stage_free, 1)

            rstds(0)
            rstds(1)
            done = 0
            for _ in range(2):
                split_lo(done)
                done += 1
            n_norm = 2
            u = 0
            for i, (kind, h, j) in enumerate(STEPS):
                if kind == "u1":
                    pool.wait_ge(silu_ok, u + 1)
                    pool.wait_ge(mask_ok, h + 1)
                    if u >= 2:
                        pool.wait_ge(drained, UNITS[u - 2] + 1)
                    nc.gpsimd.tensor_tensor(sm[:, u % 2], sg[:, u % 2],
                                            mask[:, j * P // F1, h * HALF:(h + 1) * HALF],
                                            ALU.mult).then_inc(sm_ok, 1)
                    u += 1
                if done < NSTG and kind in ("u1", "us"):
                    split_lo(done)
                    done += 1
                if kind == "u1" and h == 1 and j == 2:
                    rstds(2)
                if kind == "us" and h == 0 and j == 1:
                    rstds(3)

        @block.scalar
        def _(act):
            def split_hi(n):
                raw, hi, _ = stage_views(n)
                act.wait_ge(stage_in[n % NSTAGE], 16 * (n // NSTAGE + 1))
                nc.scalar.copy(hi, raw).then_inc(whi_ok, 1)

            def normalize(n):
                act.wait_ge(nmr_ok, n + 1)
                if n:
                    act.wait_ge(z_ok, T_STEPS[n - 1] + 1)
                for t in range(TH):
                    g = TH * (n % 2) + t
                    nc.scalar.activation(xn[:, t], xs[:, g], ACT.Identity, bias=nmr[:, g:g + 1],
                                         scale=rstd[:, g:g + 1]).then_inc(xn_ok, 1)

            normalize(0)
            split_hi(0)
            done = 1
            u = 0
            pending = []

            def split_h(v):
                act.wait_ge(drained, UNITS[v] + 1)
                if v >= 3:
                    act.wait_ge(down_ok, v - 2)
                nc.scalar.copy(h_hi[:, v % 3], hf[:, v % 2]).then_inc(hhi_ok, 1)

            for i, (kind, h, j) in enumerate(STEPS):
                s = slot[i % 2]
                act.wait_ge(z_ok, i + 1)
                if kind == "t":
                    n = t_index(i)
                    cols = slice(h * HALF, (h + 1) * HALF)
                    for k in range(KD):
                        nc.scalar.copy(xt_hi[:, k, cols], s[k][:]).then_inc(thi_ok, 1)
                    if n == 0:
                        normalize(1)
                        split_hi(1)
                        done = 2
                elif kind == "r":
                    act.wait_ge(lg_ok, 1)
                    nc.scalar.activation(ee[:], lg[:], ACT.Exp).then_inc(exp_ok, 1)
                    nc.scalar.activation(eg[:], s[0][:, 0:NT * GW].rearrange("p (t g) -> p t g", g=GW)[:, :, E2],
                                         ACT.Exp, scale=-1.0).then_inc(exp_ok, 1)
                elif kind == "c":
                    for g in range(2):
                        nc.scalar.copy(ct_hi[:, g * HALF:(g + 1) * HALF], s[g][0:E2, :]).then_inc(cthi_ok, 1)
                else:
                    if u == 0:
                        act.wait_ge(sel_ok, 3)
                    if u >= 2:
                        act.wait_ge(drained, UNITS[u - 2] + 1)
                    nc.scalar.activation(sg[:, u % 2], s[0][:], ACT.Silu).then_inc(silu_ok, 1)
                    pending.append(u)
                    u += 1
                if len(pending) > 1 or (pending and kind in "trc"):
                    split_h(pending.pop(0))
                if done < NSTG and kind in ("u1", "us"):
                    split_hi(done)
                    done += 1
                if i == NORM_STEP[2]:
                    normalize(2)
                if i == NORM_STEP[3]:
                    normalize(3)
                if i == 1:
                    act.wait_ge(g_in, 16)
                    nc.scalar.copy(g_hi[:], g_raw[:]).then_inc(ghi_ok, 1)
            for v in pending:
                split_h(v)

        @block.vector
        def _(dve):
            links = [0]

            def link(ins):
                links[0] += 1
                ins.then_inc(chain, 1)
                dve.wait_ge(chain, links[0])

            def statistics(n):
                t0 = TH * (n % 2)
                if n < 2:
                    dve.wait_ge(x_in[n], 16)
                for t in range(t0, t0 + TH):
                    last = nc.vector.bn_stats(st[:, t], xs[:, t])
                link(last)
                for t in range(t0, t0 + TH):
                    last = nc.vector.bn_aggr(mv[:, t], st[:, t])
                link(last)
                nc.vector.tensor_scalar(ve[:, t0:t0 + TH], mv[:, t0:t0 + TH, 1], EPS, None,
                                        ALU.add).then_inc(ve_ok, 1)
                dve.wait_ge(rstd_ok, n + 1)
                nc.vector.scalar_tensor_tensor(nmr[:, t0:t0 + TH], mv[:, t0:t0 + TH, 0], -1.0,
                                               rstd[:, t0:t0 + TH], ALU.mult, ALU.mult).then_inc(nmr_ok, 1)

            def masks(h):
                cols = slice(h * HALF, (h + 1) * HALF)
                dve.wait_ge(ids_in[h], 16)
                link(nc.vector.tensor_scalar(eid[:], idb[:], float(VOCAB // E1), None, ALU.is_ge))
                link(nc.vector.scalar_tensor_tensor(eid[:], idb[:], float(2 * (VOCAB // E1)), eid[:],
                                                    ALU.is_ge, ALU.add))
                nc.vector.scalar_tensor_tensor(eid[:], idb[:], float(3 * (VOCAB // E1)), eid[:],
                                               ALU.is_ge, ALU.add).then_inc(ids_used, 1)
                dve.wait_ge(ids_used, h + 1)
                for e in range(E1):
                    last = nc.vector.tensor_scalar(mask[:, e, cols], eid[:], float(e), None, ALU.is_equal)
                last.then_inc(mask_ok, 1)
                dve.wait_ge(mask_ok, h + 1)

            def split_h(v):
                dve.wait_ge(hhi_ok, v + 1)
                nc.vector.tensor_tensor(h_lo[:, v % 3], hf[:, v % 2], h_hi[:, v % 3].bitcast(F32),
                                        ALU.subtract).then_inc(hlo_ok, 1)

            def drain_y(g, h):
                dve.wait_ge(down_ok, GROUP_END[g] + 1)
                for t in range(TH):
                    n = h * TH + t
                    y = yb[t // 2][:, t % 2]
                    if g in (2, 3):
                        ins = nc.vector.scalar_tensor_tensor(xs[:, n], y, gs[:, n:n + 1], xs[:, n],
                                                             ALU.mult, ALU.add)
                    else:
                        ins = nc.vector.tensor_tensor(xs[:, n], y, xs[:, n], ALU.add)
                    if g >= 4:
                        ins.then_inc(out_ok, 1)
                if g < 4:
                    ins.then_inc(y_free, 1)

            statistics(0)
            statistics(1)
            masks(0)
            u = 0
            pending = []
            for i, (kind, h, j) in enumerate(STEPS):
                s = slot[i % 2]
                dve.wait_ge(z_ok, i + 1)
                if kind == "t":
                    n = t_index(i)
                    cols = slice(h * HALF, (h + 1) * HALF)
                    for k in range(KD):
                        dve.wait_ge(thi_ok, KD * n + k + 1)
                        last = nc.vector.tensor_tensor(xt_lo[:, k, cols], s[k][:],
                                                       xt_hi[:, k, cols].bitcast(F32), ALU.subtract)
                    last.then_inc(drained, 1)
                    if n == 1:
                        masks(1)
                        dve.wait_ge(ghi_ok, 1)
                        nc.vector.tensor_tensor(g_lo[:], g_raw[:], g_hi[:].bitcast(F32),
                                                ALU.subtract).then_inc(g_ok, 1)
                elif kind == "r":
                    logit = s[0][:, 0:NT * GW].rearrange("p (t g) -> p t g", g=GW)
                    link(nc.vector.tensor_reduce(mx[:], logit[:, :, 0:E2], AX.X, ALU.max))
                    nc.vector.tensor_tensor(lg[:], logit[:, :, 0:E2],
                                            mx[:].unsqueeze(2).broadcast_to([P, NT, E2]),
                                            ALU.subtract).then_inc(lg_ok, 1)
                    dve.wait_ge(exp_ok, 2)
                    nc.vector.tensor_scalar(gs[:], eg[:], 1.0, None, ALU.add).then_inc(drained, 1)
                    dve.wait_ge(drained, i + 1)
                    link(nc.vector.reciprocal(gs[:], gs[:]))
                    link(nc.vector.tensor_reduce(es[:], ee[:], AX.X, ALU.add))
                    link(nc.vector.reciprocal(es[:], es[:]))
                    for t in range(NT):
                        last = nc.vector.max(m8[:, t], ee[:, t])
                    link(last)
                    for t in range(NT):
                        last = nc.vector.max_index(i8[:, t], m8[:, t], ee[:, t])
                    link(last)
                    link(nc.vector.tensor_copy(i8f[:], i8[:]))
                    for t in range(NT):
                        last = nc.vector.tensor_scalar(comb[:, t], iota8[:], i8f[:, t, 0:1], None, ALU.is_equal)
                    link(last)
                    for t in range(NT):
                        last = nc.vector.scalar_tensor_tensor(comb[:, t], iota8[:], i8f[:, t, 1:2], comb[:, t],
                                                              ALU.is_equal, ALU.add)
                    link(last)
                    for t in range(NT):
                        last = nc.vector.scalar_tensor_tensor(comb[:, t], comb[:, t], es[:, t:t + 1], ee[:, t],
                                                              ALU.mult, ALU.mult)
                    last.then_inc(comb_ok, 1)
                elif kind == "c":
                    for g in range(2):
                        dve.wait_ge(cthi_ok, g + 1)
                        cols = slice(g * HALF, (g + 1) * HALF)
                        last = nc.vector.tensor_tensor(ct_lo[:, cols], s[g][0:E2, :],
                                                       ct_hi[:, cols].bitcast(F32), ALU.subtract)
                    last.then_inc(drained, 1)
                else:
                    dve.wait_ge(silu_ok, u + 1)
                    if kind == "u1":
                        dve.wait_ge(sm_ok, u + 1)
                        a, b = sm[:, u % 2], s[0]
                    elif kind == "us":
                        a, b = sg[:, u % 2], s[1]
                    else:
                        link(nc.vector.tensor_tensor(sm[:, u % 2], sg[:, u % 2], s[2][:], ALU.mult))
                        a, b = sm[:, u % 2], s[1]
                    if u >= 2:
                        dve.wait_ge(hlo_ok, u - 1)
                    nc.vector.tensor_tensor(hf[:, u % 2], a, b[:],
                                            ALU.mult).then_inc(drained, 1)
                    pending.append(u)
                    u += 1
                if len(pending) > 1 or (pending and kind in "trc"):
                    split_h(pending.pop(0))
                for g, end in enumerate(GROUP_END):
                    if i == UNITS[end] + LAG and i < len(STEPS) - 1:
                        drain_y(g, STEPS[UNITS[end]][1])
                        if g < 2:
                            dve.wait_ge(y_free, g + 1)
                        if g < 2:
                            statistics(2 + g)
            for v in pending:
                split_h(v)
            drain_y(len(GROUP_END) - 1, 1)

        @block.tensor
        def _(pe):
            def three(ps, lhs, rhs, start, stop):
                (lh, ll), (rh, rl) = lhs, rhs
                nc.tensor.matmul(ps, lh, rh, start=start, stop=False, skip_group_check=True)
                nc.tensor.matmul(ps, lh, rl, start=False, stop=False, skip_group_check=True)
                return nc.tensor.matmul(ps, ll, rh, start=False, stop=stop, skip_group_check=True)

            def down(u):
                kind, h, j = STEPS[UNITS[u]]
                pe.wait_ge(hlo_ok, u + 1)
                g = group_of(u)
                if first_of_group(u) and g == 5:
                    pe.wait_ge(out_ok, TH)
                elif first_of_group(u) and g:
                    pe.wait_ge(y_free, g)
                for t in range(TH):
                    cols = slice(t * P, t * P + P)
                    if kind == "u1":
                        w = [a[:, j * P // F1, j % KD, :] for a in (w1_hi, w1_lo)]
                    else:
                        tile = NJX + j if kind == "us" else j
                        w = [a[:, tile, 2 * D:3 * D] for a in (w2_hi, w2_lo)]
                    last = three(yb[t // 2][:, t % 2], [a[:, u % 3, cols] for a in (h_hi, h_lo)], w,
                                 first_of_group(u) and t % 2 == 0, ends_group(u))
                last.then_inc(down_ok, 1)

            pe.wait_ge(consts, 2)
            for i, (kind, h, j) in enumerate(STEPS):
                s = slot[i % 2]
                if i >= 2:
                    pe.wait_ge(drained, i - 1)
                cols = slice(h * HALF, (h + 1) * HALF)
                if kind == "t":
                    n = t_index(i)
                    pe.wait_ge(xn_ok, TH * (n + 1))
                    for k in range(KD):
                        for t in range(TH):
                            last = nc.tensor.transpose(s[k][:, t * P:t * P + P], xn[:, t, k * P:k * P + P],
                                                       ident[:])
                elif kind == "r":
                    pe.wait_ge(drained, T_STEPS[3] + 1)
                    pe.wait_ge(g_ok, 1)
                    for t in range(NT):
                        for k in range(KD):
                            last = three(s[0][:, t * GW:t * GW + NG],
                                         [a[:, k, t * P:t * P + P] for a in (xt_hi, xt_lo)],
                                         [a[:, k, :] for a in (g_hi, g_lo)], k == 0, k == KD - 1)
                elif kind == "c":
                    pe.wait_ge(comb_ok, 1)
                    for t in range(NT):
                        last = nc.tensor.transpose(s[t // TH][0:E2, (t % TH) * P:(t % TH) * P + P],
                                                   comb[:, t], ident[:])
                else:
                    if kind == "u1":
                        pe.wait_ge(drained, T_STEPS[h] + 1)
                        pe.wait_ge(stage_free, j * P // F1 + 1)
                        tiles = [(0, [[a[:, j * P // F1, k, (j % 2) * P:(j % 2) * P + P] for a in (w1_hi, w1_lo)]
                                      for k in range(KD)])]
                    else:
                        pe.wait_ge(drained, T_STEPS[2 + h] + 1)
                        pe.wait_ge(stage_free, w2_ready(kind, j))
                        tile = NJX + j if kind == "us" else j
                        tiles = [(b, [[a[:, tile, b * D + k * P:b * D + k * P + P] for a in (w2_hi, w2_lo)]
                                      for k in range(KD)]) for b in range(2)]
                    for b, w in tiles:
                        for k in range(KD):
                            last = three(s[b][:], w[k], [a[:, k, cols] for a in (xt_hi, xt_lo)],
                                         k == 0, k == KD - 1)
                    if kind == "ux":
                        pe.wait_ge(sel_ok, 3)
                        pe.wait_ge(drained, STEPS.index(("c", 0, 0)) + 1)
                        nc.tensor.matmul(s[2][:], sel[:, j * P:j * P + P], ct_hi[:, cols], start=True, stop=False)
                        last = nc.tensor.matmul(s[2][:], sel[:, j * P:j * P + P], ct_lo[:, cols],
                                                start=False, stop=True)
                last.then_inc(z_ok, 1)
                for u in downs_after(i):
                    down(u)


GROUP_END = [u for u in range(len(UNITS)) if ends_group(u)]
NORM_STEP = {2: UNITS[GROUP_END[0]] + LAG + 1, 3: UNITS[GROUP_END[1]] + LAG + 1}


def kernel(**inputs):
    import numpy as np
    import concourse.bacc as bacc
    from concourse import mybir as mb
    from concourse.bass_utils import run_bass_kernel_spmd

    x = np.ascontiguousarray(inputs["x"]).reshape(TOK, D)
    ids = np.ascontiguousarray(inputs["itok_BxS_13_99985"]).reshape(TOK)
    ctx_t = np.ascontiguousarray(np.asarray(inputs["ctx_2048"]).reshape(E1, F1, KD, P).transpose(3, 0, 2, 1))

    def join(expert, shared):
        a = np.zeros((NJ2 * P, D), np.float32)
        a[:E2 * F2] = np.asarray(expert).reshape(E2 * F2, D)
        a[NJX * P:NJX * P + FS] = np.asarray(shared)
        return a

    fc1 = join(inputs["L0_ffn_expert_fc1"], inputs["L0_ffn_shared_fc1"])
    fc2 = join(inputs["L0_ffn_expert_fc2"], inputs["L0_ffn_shared_fc2"])
    proj = join(np.asarray(inputs["L0_ffn_expert_proj"]).transpose(0, 2, 1),
                np.asarray(inputs["L0_ffn_shared_proj"]).T)
    w2 = np.zeros((NJ2, P, WT), np.float32)
    for b, fc in enumerate((fc1, fc2)):
        w2[:, :, b * D:(b + 1) * D] = fc.reshape(NJ2, P, KD, P).transpose(0, 3, 2, 1).reshape(NJ2, P, D)
    w2[:, :, 2 * D:] = proj.reshape(NJ2, P, D)
    gate = np.zeros((P, KD, NG), np.float32)
    gate[:, :, :E2] = np.asarray(inputs["L0_ffn_gate_w"]).reshape(E2, KD, P).transpose(2, 1, 0)
    gate[:, :, E2] = np.asarray(inputs["L0_ffn_shared_gate_w"]).reshape(KD, P).T

    nc = bacc.Bacc("TRN2", target_bir_lowering=False, num_devices=1)
    arrays = {"x_in_dram": x, "ids_dram": ids, "ctx_t_dram": ctx_t, "w2_dram": w2, "gate_dram": gate}
    args = [nc.dram_tensor(k, a.shape, mb.dt.from_np(a.dtype), kind="ExternalInput").ap() for k, a in arrays.items()]
    out = nc.dram_tensor("out_dram", (TOK, D), mb.dt.float32, kind="ExternalOutput").ap()
    program(nc, *args, out)
    r = run_bass_kernel_spmd(nc, [arrays], core_ids=[0])
    return r.results[0]["out_dram"].reshape(inputs["x"].shape)
```

```python
from contextlib import ExitStack

import concourse.bass as bass
from concourse import mybir

ALU = mybir.AluOpType
ACT = mybir.ActivationFunctionType
AX = mybir.AxisListType
F32 = mybir.dt.float32
F32R = mybir.dt.float32r
BF16 = mybir.dt.bfloat16
I32 = mybir.dt.int32
U32 = mybir.dt.uint32

P = 128
D = 256
KD = D // P
TOK = 1024
NT = TOK // P
HALF = 512
TH = HALF // P
E1 = 4
F1 = 256
VOCAB = 12500
E2 = 8
F2 = 176
FS = 704
NJ1 = E1 * F1 // P
NJS = -(-FS // P)
WT = 3 * D
NB = F2 // 2
WU = KD * 2 * F2
WD = 2 * D
WX = WU + WD
NX = 2 * TOK // P + E2 - 1
ROW = D + 2
OOB = 4096.0
GW = 16
NG = 10
EPS = 1e-5
LAG = 2
NSTAGE = 2
CH = 4
LOADS = [(c, min(CH, NX - c)) for c in range(0, NX, CH)]


def schedule():
    h1 = [("u1", 0, j) for j in range(NJ1)], [("u1", 1, j) for j in range(NJ1)]
    sh = [("us", 0, j) for j in range(NJS)], [("us", 1, j) for j in range(NJS)]
    return ([("t", 0, 0), ("t", 1, 0)] + h1[0] + h1[1][:6] + [("t", 0, 0)] + h1[1][6:]
            + sh[0][:3] + [("t", 1, 0), ("r", 0, 0)] + sh[0][3:] + [("p", 0, 0)] + sh[1])


STEPS = schedule()
UNITS = [i for i, s in enumerate(STEPS) if s[0][0] == "u"]
T_STEPS = [i for i, s in enumerate(STEPS) if s[0] == "t"]


def ends_group(u):
    kind, _, j = STEPS[UNITS[u]]
    return j % (F1 // P) == F1 // P - 1 if kind == "u1" else j == NJS - 1


GROUP_END = [u for u in range(len(UNITS)) if ends_group(u)]
NG1 = 2 * E1
NORM_STEP = {n: UNITS[GROUP_END[E1 * (n - 1) - 1]] + LAG + 1 for n in (2, 3)}


def downs_after(i):
    n = len(STEPS)
    if i < n - 1:
        return [u for u, s in enumerate(UNITS) if s + LAG == i]
    return [u for u, s in enumerate(UNITS) if s + LAG >= i]


def group_of(u):
    return sum(ends_group(v) for v in range(u))


def first_of_group(u):
    return u == 0 or ends_group(u - 1)


def units_until(i):
    return sum(s < i for s in UNITS)


def t_index(i):
    return sum(s[0] == "t" for s in STEPS[:i])


def program(nc, x, ids, ctx_t, ws, wx, gate, out):
    with ExitStack() as ctx:
        def sb(name, shape, dt):
            return ctx.enter_context(nc.sbuf_tensor(name, shape, dt))

        def sem(name):
            return ctx.enter_context(nc.semaphore(name))

        w_hi = sb("w_hi", [P, E2 * WX], F32R)
        w_lo = sb("w_lo", [P, E2 * WX], F32R)
        W1 = E1 * KD * F1
        w1_hi, w1_lo = [w[:, E2 * WX - W1:].rearrange("p (e k f) -> p e k f", e=E1, k=KD) for w in (w_hi, w_lo)]
        wx_hi, wx_lo = [w[:].rearrange("p (e c) -> p e c", e=E2) for w in (w_hi, w_lo)]
        ws_hi = sb("ws_hi", [P, NJS, WT], F32R)
        ws_lo = sb("ws_lo", [P, NJS, WT], F32R)
        g_raw = sb("g_raw", [P, KD, NG], F32)
        g_hi = sb("g_hi", [P, KD, NG], F32R)
        g_lo = sb("g_lo", [P, KD, NG], F32R)
        stage = sb("stage", [P, NSTAGE, WX], F32)
        xs = sb("xs", [P, NT, D], F32)
        xn = sb("xn", [P, NT, ROW], F32)
        xt_hi = sb("xt_hi", [P, KD, TOK], F32R)
        xt_lo = sb("xt_lo", [P, KD, TOK], F32R)
        idt = sb("idt", [P, NT], I32)
        eid = sb("eid", [P, NT], F32)
        mask = sb("mask", [P, E1, NT], F32)
        work = sb("work", [P, 6, HALF], F32)
        PAIRS = work[:].rearrange("p (q t) c -> p q t c", q=3)
        sg = work[:, 0:2]
        hf = work[:, 2:4]
        h_hi = sb("h_hi", [P, 3, HALF], F32R)
        h_lo = sb("h_lo", [P, 3, HALF], F32R)
        xr = sb("xr", [P, 2, CH, ROW], F32)
        xp_hi, xp_lo = [a[:, :, 0:D].rearrange("p r (k n) -> p r k n", k=KD) for a in (h_hi, h_lo)]
        hp_hi, hp_lo = [a[0:NB, :, D:2 * D].rearrange("p r (b n) -> p r b n", b=2) for a in (h_hi, h_lo)]
        sp_ = sb("sp_", [P, 2, F2], F32)
        hp = sb("hp", [P, 2, F2], F32)
        yp = sb("yp", [P, 3, D], F32)
        fill = sb("fill", [P, ROW], F32)
        ident = sb("ident", [P, P], F32)
        iota8 = sb("iota8", [P, E2], F32)
        iota_j = sb("iota_j", [P, NX, E2], F32)
        upper = sb("upper", [P, P], BF16)
        ones = sb("ones", [P, P], BF16)
        ones8 = sb("ones8", [P, E2], F32)
        half_neg = sb("half_neg", [P, TH], F32)
        st = sb("st", [P, NT, 6], F32)
        mv = sb("mv", [P, NT, 2], F32)
        ve = sb("ve", [P, NT], F32)
        rstd = sb("rstd", [P, NT], F32)
        nm = sb("nm", [P, NT], F32)
        nmr = sb("nmr", [P, NT], F32)
        mx = sb("mx", [P, NT], F32)
        lg = sb("lg", [P, NT, E2], F32)
        ee = sb("ee", [P, NT, E2], F32)
        eg = sb("eg", [P, NT], F32)
        gs = sb("gs", [P, NT], F32)
        es = sb("es", [P, NT], F32)
        m8 = sb("m8", [P, NT, 8], F32)
        i8 = sb("i8", [P, NT, 8], U32)
        i8f = sb("i8f", [P, NT, 8], F32)
        prob = sb("prob", [P, NT, 2], F32)
        first = sb("first", [P, NT], F32)
        second = sb("second", [P, NT], F32)
        wt = sb("wt", [P, NT, 2], F32)
        tmp = sb("tmp", [P, NT, 2], F32)
        oh = sb("oh", [P, 2, NT, E2], F32)
        chosen = sb("chosen", [P, NT, E2], BF16)
        n_i = sb("n_i", [P, E2], I32)
        n_t = sb("n_t", [P, E2], F32)
        end_t = sb("end_t", [P, E2], F32)
        start = sb("start", [P, E2], F32)
        place_e = sb("place_e", [P, NT, E2], F32)
        place_f = sb("place_f", [P, 2, NT], F32)
        place = sb("place", [P, 2, NT], I32)
        past = sb("past", [P, NX, E2], F32)
        te = sb("te", [P, NX], F32)
        te2 = sb("te2", [P, NX], F32)
        te_i = sb("te_i", [P, NX], I32)
        row = sb("row", [P, NX], I32)
        slot = [[ctx.enter_context(nc.psum_tensor(f"slot{i}_{b}", [P, HALF], F32)) for b in range(3)]
                for i in range(2)]
        yb = [ctx.enter_context(nc.psum_tensor(f"y{b}", [P, 2, D], F32)) for b in range(TH // 2)]
        ybanks = [yb, [slot[i][2][:].rearrange("p (t d) -> p t d", t=2) for i in range(2)]]
        rows_in = nc.dram_tensor("rows_in", (NX * P, ROW), F32).ap()
        rows_out = nc.dram_tensor("rows_out", (2 * TOK, D), F32).ap()

        x_in = [sem(f"x_in{h}") for h in range(2)]
        g_in = sem("g_in")
        ids_in = sem("ids_in")
        stage_in = [sem(f"stage_in{i}") for i in range(NSTAGE)]
        consts = sem("consts")
        fill_ok = sem("fill_ok")
        filled = sem("filled")
        lo_ok = sem("lo_ok")
        whi_ok = sem("whi_ok")
        ghi_ok = sem("ghi_ok")
        g_ok = sem("g_ok")
        ve_ok = sem("ve_ok")
        rstd_ok = sem("rstd_ok")
        nmr_ok = sem("nmr_ok")
        xn_ok = sem("xn_ok")
        z_ok = sem("z_ok")
        drained = sem("drained")
        thi_ok = sem("thi_ok")
        silu_ok = sem("silu_ok")
        hhi_ok = sem("hhi_ok")
        hlo_ok = sem("hlo_ok")
        down_ok = sem("down_ok")
        y_free = sem("y_free")
        lg_ok = sem("lg_ok")
        exp_ok = sem("exp_ok")
        chosen_ok = sem("chosen_ok")
        place_ok = sem("place_ok")
        tiles_ok = sem("tiles_ok")
        sent = sem("sent")
        rows_ok = [sem(f"rows_ok{i}") for i in range(2)]
        xt_ok = sem("xt_ok")
        xhi_ok = sem("xhi_ok")
        xlo_ok = sem("xlo_ok")
        up_ok = sem("up_ok")
        sp_ok = sem("sp_ok")
        hp_ok = sem("hp_ok")
        ht_ok = sem("ht_ok")
        hphi_ok = sem("hphi_ok")
        hplo_ok = sem("hplo_ok")
        yd_ok = sem("yd_ok")
        yp_ok = sem("yp_ok")
        row_ok = sem("row_ok")
        back = [sem(f"back{i}") for i in range(3)]
        pair_in = [sem(f"pair_in{i}") for i in range(3)]
        chain = sem("chain")
        out_ok = sem("out_ok")
        stored = sem("stored")

        xf = x.rearrange("(t p) d -> p t d", p=P)
        of = out.rearrange("(t p) d -> p t d", p=P)
        NSTG = E1 + NJS + E2
        LATE = NSTG - -(-W1 // WX)

        def stage_views(n):
            raw = stage[:, n % NSTAGE]
            if n < E1:
                raw = raw[:, 0:KD * F1].rearrange("p (k f) -> p k f", k=KD)
                return ctx_t[:, n], raw, w1_hi[:, n], w1_lo[:, n]
            if n < E1 + NJS:
                j = n - E1
                return ws[j], raw[:, 0:WT], ws_hi[:, j], ws_lo[:, j]
            e = n - E1 - NJS
            return wx[e], raw, wx_hi[:, e], wx_lo[:, e]

        def pair_buf(q):
            return PAIRS[:, q % 3]

        def split_done(eng, n):
            eng.wait_ge(lo_ok, n + 1)

        block = ctx.enter_context(nc.Block())

        @block.sync
        def _(sp):
            for h in range(2):
                sp.dma_start(xs[:, TH * h:TH * h + TH], xf[:, TH * h:TH * h + TH]).then_inc(x_in[h], 16)
            for n in range(NSTG):
                if n >= NSTAGE:
                    split_done(sp, n - NSTAGE)
                src, dst, _, _ = stage_views(n)
                sp.dma_start(dst, src).then_inc(stage_in[n % NSTAGE], 16)
                if n == 0:
                    sp.dma_start(idt[:], ids).then_inc(ids_in, 16)
                if n == 1:
                    sp.dma_start(g_raw[:], gate).then_inc(g_in, 16)
                if n == 3:
                    sp.wait_ge(fill_ok, 2)
                    sp.dma_start(rows_in.rearrange("(j p) c -> p j c", p=P),
                                 fill[:].unsqueeze(1).broadcast_to([P, NX, ROW])).then_inc(filled, 16)
            sp.wait_ge(sent, 16 * 2 * NT)
            for c, (j0, nj) in enumerate(LOADS):
                if c >= 2:
                    sp.wait_ge(xt_ok, LOADS[c - 1][0])
                    sp.wait_ge(row_ok, LOADS[c - 1][0])
                sp.dma_start(xr[:, c % 2, 0:nj], rows_in.rearrange("(j p) c -> p j c", p=P)[:, j0:j0 + nj])\
                    .then_inc(rows_ok[c % 2], 16)
            for i in range(3):
                sp.wait_ge(back[i], 16 * len(range(i, NX, 3)))
            pairs = rows_out.rearrange("(t p k) d -> p t (k d)", p=P, k=2)
            for q in range(NT // 2):
                if q >= 3:
                    sp.wait_ge(out_ok, 2 * (q - 2))
                sp.dma_start(pair_buf(q), pairs[:, 2 * q:2 * q + 2]).then_inc(pair_in[q % 3], 16)
            for q in range(NT // 2):
                sp.wait_ge(out_ok, 2 * q + 2)
                sp.dma_start(of[:, 2 * q:2 * q + 2], xs[:, 2 * q:2 * q + 2]).then_inc(stored, 16)
            sp.wait_ge(stored, 16 * NT // 2)

        @block.gpsimd
        def _(pool):
            nc.gpsimd.memset(half_neg[:], -0.5)
            nc.gpsimd.memset(ident[:], 0.0)
            nc.gpsimd.memset(ones8[:], 1.0)
            nc.gpsimd.memset(ones[:], 1.0)
            nc.gpsimd.memset(upper[:], 1.0)
            nc.gpsimd.memset(fill[:, 0:D], 0.0).then_inc(fill_ok, 1)
            nc.gpsimd.memset(fill[:, D:ROW], OOB).then_inc(fill_ok, 1)
            nc.gpsimd.iota(iota8[:], pattern=[[1, E2]], base=0, channel_multiplier=0,
                           allow_small_or_imprecise_dtypes=True)
            nc.gpsimd.iota(iota_j[:], pattern=[[1, NX], [0, E2]], base=0, channel_multiplier=0,
                           allow_small_or_imprecise_dtypes=True)
            nc.gpsimd.iota(xn[:, :, D], pattern=[[2 * P, NT]], base=0, channel_multiplier=2,
                           allow_small_or_imprecise_dtypes=True).then_inc(consts, 1)
            pool.wait_ge(consts, 1)
            nc.gpsimd.affine_select(out=ident[:], in_=ident[:], compare_op=ALU.not_equal, fill=1.0,
                                    base=0, pattern=[[-1, P]], channel_multiplier=1)
            nc.gpsimd.affine_select(out=upper[:], in_=upper[:], compare_op=ALU.is_gt, fill=0.0, base=0,
                                    pattern=[[1, P]], channel_multiplier=-1).then_inc(consts, 1)

            def rstds(n):
                t = TH * (n % 2)
                pool.wait_ge(ve_ok, n + 1)
                nc.gpsimd.tensor_tensor(rstd[:, t:t + TH], ve[:, t:t + TH], half_neg[:],
                                        ALU.pow).then_inc(rstd_ok, 1)
                pool.wait_ge(rstd_ok, n + 1)
                nc.gpsimd.tensor_tensor(nmr[:, t:t + TH], nm[:, t:t + TH], rstd[:, t:t + TH],
                                        ALU.mult).then_inc(nmr_ok, 1)

            def split_lo(n):
                _, raw, hi, lo = stage_views(n)
                pool.wait_ge(whi_ok, n + 1)
                nc.gpsimd.tensor_tensor(lo, raw, hi.bitcast(F32), ALU.subtract).then_inc(lo_ok, 1)

            rstds(0)
            rstds(1)
            done = 0
            for _ in range(2):
                split_lo(done)
                done += 1
            for i, (kind, h, j) in enumerate(STEPS):
                if done < LATE and kind == "u1" or done < NSTG and kind == "us" and (h, j) > (0, 1):
                    split_lo(done)
                    done += 1
                if kind == "u1" and (h, j) == (1, 0):
                    rstds(2)
                if kind == "us" and (h, j) == (0, 1):
                    rstds(3)
            pool.wait_ge(place_ok, 1)
            pool.wait_ge(filled, 16)
            for t in range(NT):
                for k in range(2):
                    nc.gpsimd.indirect_dma_start(
                        out=rows_in, out_offset=bass.IndirectOffsetOnAxis(ap=place[:, k, t:t + 1].bitcast(U32), axis=0),
                        in_=xn[:, t], in_offset=None).then_inc(sent, 16)
            for j in range(NX):
                pool.wait_ge(yp_ok, j + 1)
                pool.wait_ge(row_ok, j + 1)
                nc.gpsimd.indirect_dma_start(
                    out=rows_out, out_offset=bass.IndirectOffsetOnAxis(ap=row[:, j:j + 1].bitcast(U32), axis=0),
                    in_=yp[:, j % 3], in_offset=None, bounds_check=2 * TOK - 1, oob_is_err=False)\
                    .then_inc(back[j % 3], 16)

        @block.scalar
        def _(act):
            def split_hi(n):
                _, raw, hi, _ = stage_views(n)
                if n == LATE:
                    act.wait_ge(down_ok, 2 * NJ1)
                act.wait_ge(stage_in[n % NSTAGE], 16 * (n // NSTAGE + 1))
                nc.scalar.copy(hi, raw).then_inc(whi_ok, 1)

            def normalize(n):
                act.wait_ge(nmr_ok, n + 1)
                if n >= 2:
                    act.wait_ge(z_ok, T_STEPS[n - 2] + 1)
                for t in range(TH):
                    g = TH * (n % 2) + t
                    nc.scalar.activation(xn[:, g, 0:D], xs[:, g], ACT.Identity, bias=nmr[:, g:g + 1],
                                         scale=rstd[:, g:g + 1]).then_inc(xn_ok, 1)

            normalize(0)
            split_hi(0)
            done = 1
            u = 0
            pending = []

            def split_h(v):
                act.wait_ge(drained, UNITS[v] + 1)
                if v >= 3:
                    act.wait_ge(down_ok, v - 2)
                nc.scalar.copy(h_hi[:, v % 3], hf[:, v % 2]).then_inc(hhi_ok, 1)

            for i, (kind, h, j) in enumerate(STEPS):
                s = slot[i % 2]
                act.wait_ge(z_ok, i + 1)
                if kind == "t":
                    n = t_index(i)
                    cols = slice(h * HALF, (h + 1) * HALF)
                    for k in range(KD):
                        nc.scalar.copy(xt_hi[:, k, cols], s[k][:]).then_inc(thi_ok, 1)
                    if n == 0:
                        normalize(1)
                        split_hi(1)
                        done = 2
                elif kind == "r":
                    act.wait_ge(lg_ok, 1)
                    nc.scalar.activation(ee[:], lg[:], ACT.Exp).then_inc(exp_ok, 1)
                    nc.scalar.activation(eg[:], s[0][:, 0:NT * GW].rearrange("p (t g) -> p t g", g=GW)[:, :, E2],
                                         ACT.Exp, scale=-1.0).then_inc(exp_ok, 1)
                elif kind == "p":
                    pass
                else:
                    if u >= 2:
                        act.wait_ge(drained, UNITS[u - 2] + 1)
                    nc.scalar.activation(sg[:, u % 2], s[0][:], ACT.Silu).then_inc(silu_ok, 1)
                    pending.append(u)
                    u += 1
                if len(pending) > 1 or (pending and kind in "trp"):
                    split_h(pending.pop(0))
                if done < LATE and kind == "u1" or done < NSTG and kind == "us" and (h, j) > (0, 1):
                    split_hi(done)
                    done += 1
                if i == NORM_STEP[2]:
                    normalize(2)
                if i == NORM_STEP[3]:
                    normalize(3)
                if i == 1:
                    act.wait_ge(g_in, 16)
                    nc.scalar.copy(g_hi[:], g_raw[:]).then_inc(ghi_ok, 1)
            for v in pending:
                split_h(v)
            while done < NSTG:
                split_hi(done)
                done += 1

            def rows_hi(j):
                act.wait_ge(xt_ok, j + 1)
                if j >= 3:
                    act.wait_ge(up_ok, j - 2)
                nc.scalar.copy(xp_hi[:, j % 3], slot[j % 2][0][:, 0:D].rearrange("p (k n) -> p k n", k=KD))\
                    .then_inc(xhi_ok, 1)

            def gate_silu(j):
                act.wait_ge(up_ok, j + 1)
                if j >= 2:
                    act.wait_ge(hp_ok, j - 1)
                nc.scalar.activation(sp_[:, j % 2], slot[j % 2][1][:, 0:F2], ACT.Silu).then_inc(sp_ok, 1)

            def hidden_hi(j):
                act.wait_ge(ht_ok, j + 1)
                if j >= 3:
                    act.wait_ge(yd_ok, j - 2)
                nc.scalar.copy(hp_hi[:, j % 3], slot[j % 2][2][0:NB, 0:D].rearrange("p (b n) -> p b n", b=2))\
                    .then_inc(hphi_ok, 1)

            act.wait_ge(down_ok, len(UNITS))
            rows_hi(0)
            rows_hi(1)
            for j in range(NX + 1):
                if j < NX:
                    gate_silu(j)
                if j + 2 < NX:
                    rows_hi(j + 2)
                if j:
                    hidden_hi(j - 1)

        @block.vector
        def _(dve):
            links = [0]

            def link(ins):
                links[0] += 1
                ins.then_inc(chain, 1)
                dve.wait_ge(chain, links[0])

            def statistics(n):
                t0 = TH * (n % 2)
                if n < 2:
                    dve.wait_ge(x_in[n], 16)
                for t in range(t0, t0 + TH):
                    last = nc.vector.bn_stats(st[:, t], xs[:, t])
                link(last)
                for t in range(t0, t0 + TH):
                    last = nc.vector.bn_aggr(mv[:, t], st[:, t])
                link(last)
                nc.vector.tensor_scalar(nm[:, t0:t0 + TH], mv[:, t0:t0 + TH, 0], -1.0, None, ALU.mult)
                nc.vector.tensor_scalar(ve[:, t0:t0 + TH], mv[:, t0:t0 + TH, 1], EPS, None,
                                        ALU.add).then_inc(ve_ok, 1)

            def masks():
                dve.wait_ge(ids_in, 16)
                link(nc.vector.tensor_scalar(eid[:], idt[:], float(VOCAB // E1), None, ALU.is_ge))
                for k in (2, 3):
                    link(nc.vector.scalar_tensor_tensor(eid[:], idt[:], float(k * (VOCAB // E1)), eid[:],
                                                        ALU.is_ge, ALU.add))
                for e in range(E1):
                    last = nc.vector.tensor_scalar(mask[:, e], eid[:], float(e), None, ALU.is_equal)
                link(last)

            def split_h(v):
                dve.wait_ge(hhi_ok, v + 1)
                nc.vector.tensor_tensor(h_lo[:, v % 3], hf[:, v % 2], h_hi[:, v % 3].bitcast(F32),
                                        ALU.subtract).then_inc(hlo_ok, 1)

            def drain_y(g, h):
                dve.wait_ge(down_ok, GROUP_END[g] + 1)
                if g:
                    dve.wait_ge(y_free, g)
                for t in range(TH):
                    n = h * TH + t
                    y = ybanks[g % 2][t // 2][:, t % 2]
                    weight = mask[:, g % E1, n:n + 1] if g < NG1 else gs[:, n:n + 1]
                    ins = nc.vector.scalar_tensor_tensor(xs[:, n], y, weight, xs[:, n], ALU.mult, ALU.add)
                ins.then_inc(y_free, 1)

            statistics(0)
            statistics(1)
            masks()
            u = 0
            pending = []
            for i, (kind, h, j) in enumerate(STEPS):
                s = slot[i % 2]
                dve.wait_ge(z_ok, i + 1)
                if kind == "t":
                    n = t_index(i)
                    cols = slice(h * HALF, (h + 1) * HALF)
                    for k in range(KD):
                        dve.wait_ge(thi_ok, KD * n + k + 1)
                        last = nc.vector.tensor_tensor(xt_lo[:, k, cols], s[k][:],
                                                       xt_hi[:, k, cols].bitcast(F32), ALU.subtract)
                    last.then_inc(drained, 1)
                    if n == 1:
                        dve.wait_ge(ghi_ok, 1)
                        nc.vector.tensor_tensor(g_lo[:], g_raw[:], g_hi[:].bitcast(F32),
                                                ALU.subtract).then_inc(g_ok, 1)
                elif kind == "r":
                    logit = s[0][:, 0:NT * GW].rearrange("p (t g) -> p t g", g=GW)
                    link(nc.vector.tensor_reduce(mx[:], logit[:, :, 0:E2], AX.X, ALU.max))
                    nc.vector.tensor_tensor(lg[:], logit[:, :, 0:E2],
                                            mx[:].unsqueeze(2).broadcast_to([P, NT, E2]),
                                            ALU.subtract).then_inc(lg_ok, 1)
                    dve.wait_ge(exp_ok, 2)
                    nc.vector.tensor_scalar(gs[:], eg[:], 1.0, None, ALU.add).then_inc(drained, 1)
                    dve.wait_ge(drained, i + 1)
                    link(nc.vector.reciprocal(gs[:], gs[:]))
                    link(nc.vector.tensor_reduce(es[:], ee[:], AX.X, ALU.add))
                    link(nc.vector.reciprocal(es[:], es[:]))
                    for t in range(NT):
                        last = nc.vector.max(m8[:, t], ee[:, t])
                    link(last)
                    for t in range(NT):
                        last = nc.vector.max_index(i8[:, t], m8[:, t], ee[:, t])
                    link(last)
                    link(nc.vector.tensor_copy(i8f[:], i8[:]))
                    for k in range(2):
                        last = nc.vector.tensor_tensor(oh[:, k], iota8[:].unsqueeze(1).broadcast_to([P, NT, E2]),
                                                       i8f[:, :, k:k + 1].broadcast_to([P, NT, E2]), ALU.is_equal)
                    link(last)
                    nc.vector.tensor_tensor(chosen[:], oh[:, 0], oh[:, 1], ALU.add).then_inc(chosen_ok, 1)
                    nc.vector.tensor_tensor(xn[:, :, D + 1], i8f[:, :, 0], i8f[:, :, 1], ALU.add)
                    nc.vector.tensor_tensor(prob[:], m8[:, :, 0:2], es[:].unsqueeze(2).broadcast_to([P, NT, 2]), ALU.mult)
                    link(nc.vector.tensor_tensor(first[:], i8f[:, :, 0], i8f[:, :, 1], ALU.is_lt))
                    link(nc.vector.tensor_scalar(second[:], first[:], -1.0, 1.0, ALU.mult, ALU.add))
                    for k in range(2):
                        nc.vector.tensor_tensor(wt[:, :, k], prob[:, :, k], first[:], ALU.mult)
                        last = nc.vector.tensor_tensor(tmp[:, :, k], prob[:, :, 1 - k], second[:], ALU.mult)
                    link(last)
                    link(nc.vector.tensor_tensor(wt[:], wt[:], tmp[:], ALU.add))
                elif kind == "p":
                    count = s[1][:, 0:E2]
                    link(nc.vector.tensor_scalar(n_i[:], count, float(P - 1), None, ALU.add))
                    link(nc.vector.tensor_scalar(n_i[:], n_i[:], P.bit_length() - 1, None, ALU.arith_shift_right))
                    link(nc.vector.tensor_copy(n_t[:], n_i[:]))
                    link(nc.vector.tensor_tensor_scan(end_t[:], ones8[:], n_t[:], 0.0, ALU.mult, ALU.add))
                    link(nc.vector.tensor_tensor(start[:], end_t[:], n_t[:], ALU.subtract))
                    link(nc.vector.tensor_scalar(start[:], start[:], float(P), None, ALU.mult))
                    nc.vector.tensor_tensor(place_e[:], s[0][:, 0:NT * E2].rearrange("p (t e) -> p t e", e=E2),
                                            start[:].unsqueeze(1).broadcast_to([P, NT, E2]),
                                            ALU.add).then_inc(drained, 1)
                    dve.wait_ge(drained, i + 1)
                    for k in range(2):
                        last = nc.vector.tensor_tensor(oh[:, k], oh[:, k], place_e[:], ALU.mult)
                    link(last)
                    link(nc.vector.tensor_reduce(place_f[:], oh[:], AX.X, ALU.add))
                    nc.vector.tensor_copy(place[:], place_f[:]).then_inc(place_ok, 1)
                    link(nc.vector.tensor_tensor(past[:], end_t[:].unsqueeze(1).broadcast_to([P, NX, E2]), iota_j[:],
                                                 ALU.is_le))
                    link(nc.vector.tensor_reduce(te[:], past[:], AX.X, ALU.add))
                    link(nc.vector.tensor_scalar(te[:], te[:], float(E2 - 1), None, ALU.min))
                    nc.vector.tensor_scalar(te2[:], te[:], 2.0, None, ALU.mult)
                    nc.vector.tensor_copy(te_i[:], te[:]).then_inc(tiles_ok, 1)
                    dve.wait_ge(tiles_ok, 1)
                else:
                    dve.wait_ge(silu_ok, u + 1)
                    b = s[0] if kind == "u1" else s[1]
                    if u >= 2:
                        dve.wait_ge(hlo_ok, u - 1)
                    nc.vector.tensor_tensor(hf[:, u % 2], sg[:, u % 2], b[:],
                                            ALU.mult).then_inc(drained, 1)
                    pending.append(u)
                    u += 1
                if len(pending) > 1 or (pending and kind in "trp"):
                    split_h(pending.pop(0))
                for g, end in enumerate(GROUP_END):
                    if i == UNITS[end] + LAG and i < len(STEPS) - 1:
                        drain_y(g, STEPS[UNITS[end]][1])
                        if g in (E1 - 1, NG1 - 1):
                            dve.wait_ge(y_free, g + 1)
                            statistics(2 + g // E1)
            for v in pending:
                split_h(v)
            drain_y(NG1 + 1, 1)

            def rows_lo(j):
                dve.wait_ge(xhi_ok, j + 1)
                nc.vector.tensor_tensor(xp_lo[:, j % 3], slot[j % 2][0][:, 0:D].rearrange("p (k n) -> p k n", k=KD),
                                        xp_hi[:, j % 3].bitcast(F32), ALU.subtract).then_inc(xlo_ok, 1)

            def row_numbers(j):
                c = j // CH
                dve.wait_ge(rows_ok[c % 2], 16 * (c // 2 + 1))
                tail = xr[:, c % 2, j % CH, D:ROW]
                nc.vector.scalar_tensor_tensor(row[:, j:j + 1], tail[:, 1:2], te2[:, j:j + 1], tail[:, 0:1],
                                               ALU.is_lt, ALU.add).then_inc(row_ok, 1)

            def hidden(j):
                dve.wait_ge(sp_ok, j + 1)
                if j >= 2:
                    dve.wait_ge(ht_ok, j - 1)
                nc.vector.tensor_tensor(hp[:, j % 2], sp_[:, j % 2], slot[j % 2][1][:, F2:2 * F2],
                                        ALU.mult).then_inc(hp_ok, 1)

            def hidden_lo(j):
                dve.wait_ge(hphi_ok, j + 1)
                nc.vector.tensor_tensor(hp_lo[:, j % 3], slot[j % 2][2][0:NB, 0:D].rearrange("p (b n) -> p b n", b=2),
                                        hp_hi[:, j % 3].bitcast(F32), ALU.subtract).then_inc(hplo_ok, 1)

            def result(j):
                dve.wait_ge(yd_ok, j + 1)
                if j >= 3:
                    dve.wait_ge(back[j % 3], 16 * (j // 3))
                nc.vector.tensor_copy(yp[:, j % 3], yb[j % 2][:, 0]).then_inc(yp_ok, 1)

            rows_lo(0)
            rows_lo(1)
            for j in range(NX + 2):
                if j < NX:
                    row_numbers(j)
                    hidden(j)
                if j + 2 < NX:
                    rows_lo(j + 2)
                if 1 <= j <= NX:
                    hidden_lo(j - 1)
                if j >= 2:
                    result(j - 2)

            for t in range(NT):
                q = t // 2
                dve.wait_ge(pair_in[q % 3], 16 * (q // 3 + 1))
                pair = pair_buf(q)[:, t % 2].rearrange("p (k d) -> p k d", k=2)
                link(nc.vector.scalar_tensor_tensor(xs[:, t], pair[:, 0], wt[:, t, 0:1], xs[:, t], ALU.mult, ALU.add))
                nc.vector.scalar_tensor_tensor(xs[:, t], pair[:, 1], wt[:, t, 1:2], xs[:, t], ALU.mult,
                                               ALU.add).then_inc(out_ok, 1)

        @block.tensor
        def _(pe):
            def three(ps, lhs, rhs, start, stop):
                (lh, ll), (rh, rl) = lhs, rhs
                nc.tensor.matmul(ps, lh, rh, start=start, stop=False, skip_group_check=True)
                nc.tensor.matmul(ps, lh, rl, start=False, stop=False, skip_group_check=True)
                return nc.tensor.matmul(ps, ll, rh, start=False, stop=stop, skip_group_check=True)

            def down(u):
                kind, h, j = STEPS[UNITS[u]]
                pe.wait_ge(hlo_ok, u + 1)
                g = group_of(u)
                if first_of_group(u) and g >= 2:
                    pe.wait_ge(y_free, g - 1)
                for t in range(TH):
                    cols = slice(t * P, t * P + P)
                    if kind == "u1":
                        w = [a[:, j * P // F1, j % KD, :] for a in (w1_hi, w1_lo)]
                    else:
                        w = [a[:, j, 2 * D:3 * D] for a in (ws_hi, ws_lo)]
                    last = three(ybanks[g % 2][t // 2][:, t % 2], [a[:, u % 3, cols] for a in (h_hi, h_lo)], w,
                                 first_of_group(u) and t % 2 == 0, ends_group(u))
                last.then_inc(down_ok, 1)

            for i, (kind, h, j) in enumerate(STEPS):
                s = slot[i % 2]
                if i >= 2:
                    pe.wait_ge(drained, i - 1)
                cols = slice(h * HALF, (h + 1) * HALF)
                if kind == "t":
                    n = t_index(i)
                    pe.wait_ge(xn_ok, TH * (n + 1))
                    pe.wait_ge(consts, 2)
                    for k in range(KD):
                        for t in range(TH):
                            last = nc.tensor.transpose(s[k][:, t * P:t * P + P], xn[:, h * TH + t, k * P:k * P + P],
                                                       ident[:])
                elif kind == "r":
                    pe.wait_ge(drained, T_STEPS[3] + 1)
                    pe.wait_ge(g_ok, 1)
                    for t in range(NT):
                        for k in range(KD):
                            last = three(s[0][:, t * GW:t * GW + NG],
                                         [a[:, k, t * P:t * P + P] for a in (xt_hi, xt_lo)],
                                         [a[:, k, :] for a in (g_hi, g_lo)], k == 0, k == KD - 1)
                elif kind == "p":
                    pe.wait_ge(chosen_ok, 1)
                    flat = chosen[:].rearrange("p t e -> p (t e)")
                    nc.tensor.matmul(s[0][:, 0:NT * E2], upper[:], flat, start=True, stop=False, skip_group_check=True)
                    for d in range(1, NT):
                        nc.tensor.matmul(s[0][:, d * E2:NT * E2], ones[:], flat[:, 0:(NT - d) * E2],
                                         start=False, stop=d == NT - 1, skip_group_check=True)
                    for t in range(NT):
                        last = nc.tensor.matmul(s[1][:, 0:E2], ones[:], chosen[:, t], start=t == 0, stop=t == NT - 1)
                else:
                    if kind == "u1":
                        pe.wait_ge(drained, T_STEPS[h] + 1)
                        split_done(pe, j * P // F1)
                        tiles = [(0, [[a[:, j * P // F1, k, (j % 2) * P:(j % 2) * P + P] for a in (w1_hi, w1_lo)]
                                      for k in range(KD)])]
                    else:
                        pe.wait_ge(drained, T_STEPS[2 + h] + 1)
                        split_done(pe, E1 + j)
                        tiles = [(b, [[a[:, j, b * D + k * P:b * D + k * P + P] for a in (ws_hi, ws_lo)]
                                      for k in range(KD)]) for b in range(2)]
                    for b, w in tiles:
                        for k in range(KD):
                            last = three(s[b][:], w[k], [a[:, k, cols] for a in (xt_hi, xt_lo)],
                                         k == 0, k == KD - 1)
                last.then_inc(z_ok, 1)
                for u in downs_after(i):
                    down(u)

            def rows_t(j):
                c = j // CH
                pe.wait_ge(rows_ok[c % 2], 16 * (c // 2 + 1))
                if j < 2:
                    pe.wait_ge(drained, len(STEPS) - j % 2)
                else:
                    pe.wait_ge(xlo_ok, j - 1)
                for k in range(KD):
                    last = nc.tensor.transpose(slot[j % 2][0][:, k * P:k * P + P],
                                               xr[:, c % 2, j % CH, k * P:k * P + P], ident[:])
                last.then_inc(xt_ok, 1)

            def up(j, e):
                pe.wait_ge(xlo_ok, j + 1)
                if j >= 2:
                    pe.wait_ge(hp_ok, j - 1)
                for k in range(KD):
                    w = [a[:, bass.ds(e * WX + k * 2 * F2, 2 * F2)] for a in (w_hi, w_lo)]
                    last = three(slot[j % 2][1][:, 0:2 * F2], [a[:, j % 3, k] for a in (xp_hi, xp_lo)], w,
                                 k == 0, k == KD - 1)
                last.then_inc(up_ok, 1)

            def hidden_t(j):
                pe.wait_ge(hp_ok, j + 1)
                if j >= 2:
                    pe.wait_ge(hplo_ok, j - 1)
                else:
                    pe.wait_ge(y_free, NG1 + 2)
                for b in range(2):
                    last = nc.tensor.transpose(slot[j % 2][2][0:NB, b * P:b * P + P], hp[:, j % 2, b * NB:(b + 1) * NB],
                                               ident[:])
                last.then_inc(ht_ok, 1)

            def down_x(j, e):
                pe.wait_ge(hplo_ok, j + 1)
                if j >= 2:
                    pe.wait_ge(yp_ok, j - 1)
                else:
                    pe.wait_ge(y_free, NG1 + 2)
                for b in range(2):
                    w = [a[0:NB, bass.ds(e * WX + WU + b * D, D)] for a in (w_hi, w_lo)]
                    last = three(yb[j % 2][:, 0], [a[:, j % 3, b] for a in (hp_hi, hp_lo)], w, b == 0, b == 1)
                last.then_inc(yd_ok, 1)

            rows_t(0)
            rows_t(1)
            pe.wait_ge(tiles_ok, 1)
            split_done(pe, NSTG - 1)
            regs = [pe.alloc_register(f"expert{j}") for j in range(NX)]
            nc.tensor.load(regs, te_i[0:1, 0:NX])
            expert = {}
            for j in range(NX + 2):
                if j < NX:
                    expert[j] = nc.tensor.snap(regs[j], min_val=0, max_val=E2 - 1)
                    up(j, expert[j])
                if j + 2 < NX:
                    rows_t(j + 2)
                if 1 <= j <= NX:
                    hidden_t(j - 1)
                if j >= 2:
                    down_x(j - 2, expert[j - 2])


def kernel(**inputs):
    import numpy as np
    import concourse.bacc as bacc
    from concourse import mybir as mb
    from concourse.bass_utils import run_bass_kernel_spmd

    x = np.ascontiguousarray(inputs["x"]).reshape(TOK, D)
    ids = np.ascontiguousarray(inputs["itok_BxS_13_99985"]).reshape(TOK)
    ctx_t = np.ascontiguousarray(np.asarray(inputs["ctx_2048"]).reshape(E1, F1, KD, P).transpose(3, 0, 2, 1))

    def blocks(a):
        a = a.reshape(*a.shape[:-1], KD, P)
        return np.moveaxis(a, -3, -1).swapaxes(-3, -2)

    def padded(a):
        return np.concatenate([a, np.zeros((NJS * P - FS, D), np.float32)]).reshape(NJS, P, D)

    ws = np.zeros((NJS, P, WT), np.float32)
    for b, name in enumerate(("shared_fc1", "shared_fc2")):
        ws[:, :, b * D:(b + 1) * D] = blocks(padded(np.asarray(inputs["L0_ffn_" + name]))).reshape(NJS, P, D)
    ws[:, :, 2 * D:] = padded(np.asarray(inputs["L0_ffn_shared_proj"]).T)
    wx = np.zeros((E2, P, WX), np.float32)
    up = wx[:, :, :WU].reshape(E2, P, KD, 2, F2)
    for b, name in enumerate(("expert_fc1", "expert_fc2")):
        up[:, :, :, b] = blocks(np.asarray(inputs["L0_ffn_" + name]))
    wx[:, :, :WU] = up.reshape(E2, P, WU)
    proj = np.asarray(inputs["L0_ffn_expert_proj"]).reshape(E2, D, 2, NB)
    wx[:, :NB, WU:] = proj.transpose(0, 3, 2, 1).reshape(E2, NB, WD)
    gate = np.zeros((P, KD, NG), np.float32)
    gate[:, :, :E2] = np.asarray(inputs["L0_ffn_gate_w"]).reshape(E2, KD, P).transpose(2, 1, 0)
    gate[:, :, E2] = np.asarray(inputs["L0_ffn_shared_gate_w"]).reshape(KD, P).T

    nc = bacc.Bacc("TRN2", target_bir_lowering=False, num_devices=1)
    arrays = {"x_in_dram": x, "ids_dram": ids.reshape(NT, P).T.copy(), "ctx_t_dram": ctx_t, "ws_dram": ws, "wx_dram": wx, "gate_dram": gate}
    args = [nc.dram_tensor(k, a.shape, mb.dt.from_np(a.dtype), kind="ExternalInput").ap() for k, a in arrays.items()]
    out = nc.dram_tensor("out_dram", (TOK, D), mb.dt.float32, kind="ExternalOutput").ap()
    program(nc, *args, out)
    r = run_bass_kernel_spmd(nc, [arrays], core_ids=[0])
    return r.results[0]["out_dram"].reshape(inputs["x"].shape)
```

```python
from contextlib import ExitStack

import concourse.bass as bass
from concourse import mybir

ALU = mybir.AluOpType
ACT = mybir.ActivationFunctionType
AX = mybir.AxisListType
F32 = mybir.dt.float32
F32R = mybir.dt.float32r
BF16 = mybir.dt.bfloat16
I32 = mybir.dt.int32
U32 = mybir.dt.uint32

P = 128
D = 256
KD = D // P
TOK = 1024
NT = TOK // P
HALF = 512
TH = HALF // P
E1 = 4
F1 = 256
VOCAB = 12500
E2 = 8
F2 = 176
FS = 704
NJ1 = E1 * F1 // P
NJS = -(-FS // P)
R = P // 2
WT = 3 * D
NB = F2 // 2
WU = KD * 2 * F2
WD = 2 * D
WX = WU + WD
NX = 2 * TOK // P + E2 - 1
POST = 3
GW = 32
NG = 10
EPS = 1e-5
LAG = {"u1": 3, "us": 2}
RING = max(LAG.values()) + 1
AHEAD = 3
WARM = 50
NSTAGE = 3
LEAD = 2
RX = 8
POOL_TILES = 3
PAIRS = [4, 0, 6, 2]
STORES = [0, 4, 6, 2]


def schedule():
    h1 = [("u1", 0, j) for j in range(NJ1)], [("u1", 1, j) for j in range(NJ1)]
    sh = [("us", 0, j) for j in range(NJS)], [("us", 1, j) for j in range(NJS)]
    return ([("t", 0, 0)] + h1[0][:2] + [("t", 1, 0)] + h1[0][2:]
            + h1[1][:6] + [("t", 0, 0)] + h1[1][6:7] + [("r", 0, 0)] + h1[1][7:]
            + sh[0][:3] + [("t", 1, 0)] + sh[0][3:4] + [("r", 1, 0)] + sh[0][4:5] + [("p", 0, 0)]
            + sh[0][5:] + sh[1][:2] + [("q", 0, 0)] + sh[1][2:])


STEPS = schedule()
UNITS = [i for i, s in enumerate(STEPS) if s[0][0] == "u"]
T_STEPS = [i for i, s in enumerate(STEPS) if s[0] == "t"]
P_STEP = STEPS.index(("p", 0, 0))
Q_STEP = STEPS.index(("q", 0, 0))
E_AT = len(STEPS) - POST
NPRE = len(UNITS) - POST


def ends_group(u):
    kind, h, j = STEPS[UNITS[u]]
    return j % (F1 // P) == F1 // P - 1 if kind == "u1" else j == NJS - 1 or (h, j) == (1, NJS - 1 - POST)


def rows(u):
    return slice(R, P) if STEPS[UNITS[u]][0] == "us" and STEPS[UNITS[u]][2] == NJS - 1 else slice(0, P)


GROUP_END = [u for u in range(len(UNITS)) if ends_group(u)]
NG1 = 2 * E1


def downs():
    after, u, lag = [], 0, 0
    for i, (kind, _, _) in enumerate(STEPS):
        lag = LAG.get(kind, lag)
        end = sum(s + lag <= i for s in UNITS)
        if i == E_AT - 1:
            end = NPRE
        if i == len(STEPS) - 1:
            end = len(UNITS)
        if i == UNITS[2 * NJ1]:
            end = 2 * NJ1
        after.append(list(range(u, max(u, end))))
        u = max(u, end)
    return after


DOWNS = downs()


def group_of(u):
    return sum(ends_group(v) for v in range(u))


def first_of_group(u):
    return u == 0 or ends_group(u - 1)


def t_index(i):
    return sum(s[0] == "t" for s in STEPS[:i])


LAST_RING = NPRE - RING + 1
NSTG = E1 + NJS + E2
FIRST = 2
SPLIT_UNITS = [0, 2, 3, 5, 6, 8, 9, 11, 12, 14, 16, 17, 18, 19, 20, 21]
STORE_AFTER = 12, 14
SPLITS = {UNITS[u]: FIRST + k for k, u in enumerate(SPLIT_UNITS)}
NORM_STEP = {n: next(i for i, d in enumerate(DOWNS) if GROUP_END[E1 * (n - 1) - 1] in d) for n in (2, 3)}


def program(nc, x, ids, ctx_t, ws, wx, gate, out):
    with ExitStack() as ctx:
        def sb(name, shape, dt):
            return ctx.enter_context(nc.sbuf_tensor(name, shape, dt))

        def sem(name):
            return ctx.enter_context(nc.semaphore(name))

        w_hi = sb("w_hi", [P, E2 * WX], F32R)
        w_lo = sb("w_lo", [P, E2 * WX], F32R)
        W1 = E1 * KD * F1
        w1_hi, w1_lo = [w[:, E2 * WX - W1:].rearrange("p (e k f) -> p e k f", e=E1, k=KD) for w in (w_hi, w_lo)]
        wx_hi, wx_lo = [w[:].rearrange("p (e c) -> p e c", e=E2) for w in (w_hi, w_lo)]
        ws_hi = sb("ws_hi", [P, NJS, WT], F32R)
        ws_lo = sb("ws_lo", [P, NJS, WT], F32R)
        g_raw = sb("g_raw", [P, KD, NG], F32)
        g_hl = sb("g_hl", [P, KD, 2, NG], F32R)
        g_hi, g_lo = g_hl[:, :, 0], g_hl[:, :, 1]
        stage = sb("stage", [P, NSTAGE, WX], F32)
        xs = sb("xs", [P, NT, D], F32)
        xn = sb("xn", [P, NT, D], F32)
        xt_hi = sb("xt_hi", [P, KD, TOK], F32R)
        xt_lo = sb("xt_lo", [P, KD, TOK], F32R)
        idt = sb("idt", [P, NT], I32)
        eid = sb("eid", [P, NT], F32)
        mask = sb("mask", [P, E1, NT], F32)
        work = sb("work", [P, 4, HALF], F32)
        sg = work[:, 0:2]
        hf = work[:, 2:4]
        h_hi = sb("h_hi", [P, RING, HALF], F32R)
        h_lo = sb("h_lo", [P, RING, HALF], F32R)
        xr = sb("xr", [P, RX, D], F32)
        xp_hi, xp_lo = [a[:, :, 0:D].rearrange("p r (k n) -> p r k n", k=KD) for a in (h_hi, h_lo)]
        hp_hi, hp_lo = [a[0:NB, :, D:2 * D].rearrange("p r (b n) -> p r b n", b=2) for a in (h_hi, h_lo)]
        sp_ = sb("sp_", [P, 2, F2], F32)
        hp = sb("hp", [P, 2, F2], F32)
        yp = sb("yp", [P, 3, D], F32)
        ident = sb("ident", [P, P], F32)
        iota_j = sb("iota_j", [P, NX, E2], F32)
        upper = sb("upper", [P, P], BF16)
        ones = sb("ones", [P, P], BF16)
        ones8 = sb("ones8", [P, E2], F32)
        half_neg = sb("half_neg", [P, TH], F32)
        st = sb("st", [P, NT, 6], F32)
        mv = sb("mv", [P, NT, 2], F32)
        ve = sb("ve", [P, NT], F32)
        rstd = sb("rstd", [P, NT], F32)
        logit = sb("logit", [P, NT, NG], F32)
        lg = sb("lg", [P, NT, E2], F32)
        ee = sb("ee", [P, NT, E2], F32)
        eg = sb("eg", [P, NT], F32)
        gs = sb("gs", [P, NT], F32)
        es = sb("es", [P, NT], F32)
        m8 = sb("m8", [P, NT, 8], F32)
        top = sb("top", [P, NT, 2], F32)
        rank = sb("rank", [P, NT, E2], F32)
        lower = sb("lower", [P, E2, E2], F32)
        larger, same = [a[:].rearrange("p b f -> p (b f)")[:, 0:TH * E2 * E2]
                        .rearrange("p (t e f) -> p t e f", t=TH, e=E2) for a in (sp_, hp)]
        prob = sb("prob", [P, NT, 2], F32)
        top_lg = sb("top_lg", [P, NT, 2], F32)
        oh = sb("oh", [P, 2, NT, E2], F32)
        chosen = sb("chosen", [P, NT, E2], BF16)
        n_i = sb("n_i", [P, E2], I32)
        n_t = sb("n_t", [P, E2], F32)
        end_t = sb("end_t", [P, E2], F32)
        start = sb("start", [P, E2], F32)
        place_e = sb("place_e", [P, NT, E2], F32)
        place_f = sb("place_f", [P, 2, NT], F32)
        place = sb("place", [P, 2, NT], I32)
        past = sb("past", [P, NX, E2], F32)
        te = sb("te", [P, NX], F32)
        te_i = sb("te_i", [P, NX], I32)
        iota_p = work[:, 0, 0:P]
        iota_b = sb("iota_b", [P, P], BF16)
        val = sb("val", [P, 2, NT, 2], F32)
        place_j = sb("place_j", [P, 2 * NT], F32)
        place_p = sb("place_p", [P, 2 * NT], BF16)
        at_p = xr[:, 0:4].rearrange("p r d -> p (r d)").bitcast(BF16).rearrange("p (q m) -> p q m", q=2 * NT)
        at_j = sb("at_j", [P, 2 * NT, NX], BF16)
        at_v = sb("at_v", [P, 2 * NT, 2, NX], BF16)
        row_f = sb("row_f", [P, NX], F32)
        row = sb("row", [P, NX], I32)
        src = sb("src", [P, NX], I32)
        slot = [[ctx.enter_context(nc.psum_tensor(f"slot{i}_{b}", [P, HALF], F32)) for b in range(3)]
                for i in range(2)]
        yb = [ctx.enter_context(nc.psum_tensor(f"y{b}", [P, 2, D], F32)) for b in range(TH // 2)]
        ybanks = [yb, [slot[i][2][:].rearrange("p (t d) -> p t d", t=2) for i in range(2)]]
        rows_in = nc.dram_tensor("rows_in", (TOK + 1, D), F32).ap()
        rows_out = nc.dram_tensor("rows_out", (2 * TOK, D), F32).ap()

        x_in = [sem(f"x_in{q}") for q in range(NT // 2)]
        g_in = sem("g_in")
        ids_in = sem("ids_in")
        stage_in = [sem(f"stage_in{i}") for i in range(NSTAGE)]
        consts = sem("consts")
        lo_ok = sem("lo_ok")
        whi_ok = sem("whi_ok")
        ghi_ok = sem("ghi_ok")
        g_ok = sem("g_ok")
        ve_ok = sem("ve_ok")
        rstd_ok = sem("rstd_ok")
        xn_ok = sem("xn_ok")
        z_ok = sem("z_ok")
        drained = sem("drained")
        thi_ok = sem("thi_ok")
        silu_ok = sem("silu_ok")
        hhi_ok = sem("hhi_ok")
        hlo_ok = sem("hlo_ok")
        down_ok = sem("down_ok")
        y_free = sem("y_free")
        lg_ok = sem("lg_ok")
        exp_ok = sem("exp_ok")
        chosen_ok = sem("chosen_ok")
        tiles_ok = sem("tiles_ok")
        hot_ok = sem("hot_ok")
        src_ok = sem("src_ok")
        sent = sem("sent")
        rows_ok = [sem(f"rows_ok{i}") for i in range(RX)]
        xt_ok = sem("xt_ok")
        xhi_ok = sem("xhi_ok")
        xlo_ok = sem("xlo_ok")
        up_ok = sem("up_ok")
        sp_ok = sem("sp_ok")
        hp_ok = sem("hp_ok")
        ht_ok = sem("ht_ok")
        hphi_ok = sem("hphi_ok")
        hplo_ok = sem("hplo_ok")
        yd_ok = sem("yd_ok")
        yp_ok = sem("yp_ok")
        back = [sem(f"back{i}") for i in range(3)]
        pair_in = [sem(f"pair_in{t}") for t in range(NT)]
        chain = sem("chain")
        scaled = sem("scaled")
        added = sem("added")
        pool_ok = sem("pool_ok")
        out_ok = sem("out_ok")
        stored = sem("stored")

        xf = x.rearrange("(t p) d -> p t d", p=P)
        of = out.rearrange("(t p) d -> p t d", p=P)
        LATE = NSTG - -(-W1 // WX)

        def ring(j):
            return (NPRE + j % 3) % RING

        def stage_views(n):
            raw = stage[:, n % NSTAGE]
            if n < E1:
                raw = raw[:, 0:KD * F1].rearrange("p (k f) -> p k f", k=KD)
                return ctx_t[:, n], raw, w1_hi[:, n], w1_lo[:, n]
            if n < E1 + NJS:
                j = n - E1
                return ws[j], raw[:, 0:WT], ws_hi[:, j], ws_lo[:, j]
            e = n - E1 - NJS
            return wx[e], raw, wx_hi[:, e], wx_lo[:, e]

        def pair_buf(t):
            q = PAIRS.index(t)
            if q < NSTAGE:
                return stage[:, q, 0:4 * D].rearrange("p (t c) -> p t c", t=2)
            return xr[:, 0:4].rearrange("p (t k) c -> p t (k c)", t=2)

        def split_done(eng, n):
            eng.wait_ge(lo_ok, n + 1)

        block = ctx.enter_context(nc.Block())

        @block.sync
        def _(sp):
            def load_x(h):
                for q in range(h * TH // 2, (h + 1) * TH // 2):
                    sp.dma_start(xs[:, 2 * q:2 * q + 2], xf[:, 2 * q:2 * q + 2]).then_inc(x_in[q], 16)

            load_x(0)
            for n in range(NSTG):
                if n >= NSTAGE:
                    split_done(sp, n - NSTAGE)
                src, dst, _, _ = stage_views(n)
                sp.dma_start(dst, src).then_inc(stage_in[n % NSTAGE], 16)
                if n == 0:
                    load_x(1)
                    sp.dma_start(idt[:], ids).then_inc(ids_in, 16)
                if n == 1:
                    sp.dma_start(g_raw[:], gate).then_inc(g_in, 16)
                for h in range(2):
                    if n == STORE_AFTER[h]:
                        sp.wait_ge(xn_ok, (h + 3) * TH)
                        t = h * TH
                        sp.dma_start(rows_in[0:TOK].rearrange("(t p) d -> p t d", p=P)[:, t:t + TH],
                                     xn[:, t:t + TH]).then_inc(sent, 16)
            sp.dma_start(rows_in[TOK:TOK + 1], xn[0:1, 0]).then_inc(sent, 16)
            for i in range(3):
                sp.wait_ge(back[i], 16 * len(range(i, NX, 3)))
            pairs = rows_out.rearrange("(t p k) d -> p t (k d)", p=P, k=2)
            sp.wait_ge(xt_ok, NX)
            for t in PAIRS:
                sp.dma_start(pair_buf(t), pairs[:, t:t + 2]).then_inc(pair_in[t], 16)
            for t in STORES:
                if t >= TH:
                    sp.wait_ge(out_ok, t - TH + 2)
                else:
                    sp.wait_ge(pool_ok, 2 * min(t + 2, POOL_TILES))
                    if t + 2 > POOL_TILES:
                        sp.wait_ge(added, 2 * (NT - POOL_TILES))
                sp.dma_start(of[:, t:t + 2], xs[:, t:t + 2]).then_inc(stored, 16)
            sp.wait_ge(stored, 16 * NT // 2)

        @block.gpsimd
        def _(pool):
            nc.gpsimd.memset(half_neg[:], -0.5)
            nc.gpsimd.memset(ident[:], 0.0)
            nc.gpsimd.memset(ones8[:], 1.0)
            nc.gpsimd.memset(ones[:], 1.0)
            nc.gpsimd.memset(upper[:], 1.0)
            nc.gpsimd.memset(lower[:], 1.0)
            nc.gpsimd.iota(iota_j[:], pattern=[[1, NX], [0, E2]], base=0, channel_multiplier=0,
                           allow_small_or_imprecise_dtypes=True)
            nc.gpsimd.iota(val[:, :, :, 0], pattern=[[0, 2], [-1, NT]], base=NT, channel_multiplier=0,
                           allow_small_or_imprecise_dtypes=True)
            nc.gpsimd.iota(val[:, :, :, 1], pattern=[[1, 2], [0, NT]], base=0, channel_multiplier=2,
                           allow_small_or_imprecise_dtypes=True)
            nc.gpsimd.iota(iota_p, pattern=[[1, P]], base=0, channel_multiplier=0,
                           allow_small_or_imprecise_dtypes=True).then_inc(consts, 1)
            pool.wait_ge(consts, 1)
            nc.gpsimd.tensor_copy(iota_b[:], iota_p)
            nc.gpsimd.affine_select(out=ident[:], in_=ident[:], compare_op=ALU.not_equal, fill=1.0,
                                    base=0, pattern=[[-1, P]], channel_multiplier=1)
            nc.gpsimd.affine_select(out=lower[:], in_=lower[:], compare_op=ALU.is_gt, fill=0.0, base=0,
                                    pattern=[[1, E2], [-1, E2]], channel_multiplier=0)
            nc.gpsimd.affine_select(out=upper[:], in_=upper[:], compare_op=ALU.is_gt, fill=0.0, base=0,
                                    pattern=[[1, P]], channel_multiplier=-1).then_inc(consts, 1)

            def rstds(n):
                t = TH * (n % 2)
                pool.wait_ge(ve_ok, n + 1)
                nc.gpsimd.tensor_tensor(rstd[:, t:t + TH], ve[:, t:t + TH], half_neg[:],
                                        ALU.pow).then_inc(rstd_ok, 1)

            def split_lo(n):
                _, raw, hi, lo = stage_views(n)
                pool.wait_ge(whi_ok, n + 1)
                nc.gpsimd.tensor_tensor(lo, raw, hi.bitcast(F32), ALU.subtract).then_inc(lo_ok, 1)

            def gather(j):
                if j >= RX:
                    pool.wait_ge(xt_ok, j - RX + 1)
                nc.gpsimd.indirect_dma_start(
                    out=xr[:, j % RX], out_offset=None, in_=rows_in,
                    in_offset=bass.IndirectOffsetOnAxis(ap=src[:, j:j + 1].bitcast(U32), axis=0))\
                    .then_inc(rows_ok[j % RX], 16)

            rstds(0)
            split_lo(0)
            rstds(1)
            split_lo(1)
            for i in range(len(STEPS)):
                for n in (2, 3):
                    if i == NORM_STEP[n]:
                        rstds(n)
                if i in SPLITS:
                    split_lo(SPLITS[i])
            pool.wait_ge(src_ok, 1)
            pool.wait_ge(sent, 16 * 3)
            for j in range(RX + LEAD):
                gather(j)
            for j in range(NX):
                if j + RX + LEAD < NX:
                    gather(j + RX + LEAD)
                pool.wait_ge(yp_ok, j + 1)
                nc.gpsimd.indirect_dma_start(
                    out=rows_out, out_offset=bass.IndirectOffsetOnAxis(ap=row[:, j:j + 1].bitcast(U32), axis=0),
                    in_=yp[:, j % 3], in_offset=None, bounds_check=2 * TOK - 1, oob_is_err=False)\
                    .then_inc(back[j % 3], 16)
            pool.wait_ge(y_free, NG1 + 1)
            for n, (t, k) in enumerate([(t, k) for t in range(POOL_TILES) for k in range(2)]):
                pool.wait_ge(scaled, n + 1)
                if k:
                    pool.wait_ge(pool_ok, n)
                nc.gpsimd.tensor_tensor(xs[:, t], pair_buf(t - t % 2)[:, t % 2, k * D:(k + 1) * D], xs[:, t],
                                        ALU.add).then_inc(pool_ok, 1)

        @block.scalar
        def _(act):
            def split_hi(n):
                _, raw, hi, _ = stage_views(n)
                if n == LATE:
                    act.wait_ge(down_ok, 2 * NJ1)
                act.wait_ge(stage_in[n % NSTAGE], 16 * (n // NSTAGE + 1))
                nc.scalar.copy(hi, raw).then_inc(whi_ok, 1)

            split_hi(0)
            u = 0
            pending = []

            def split_h(v):
                act.wait_ge(drained, UNITS[v] + 1)
                if v >= RING:
                    act.wait_ge(down_ok, v - RING + 1)
                if v == NPRE:
                    act.wait_ge(yd_ok, NX)
                    act.wait_ge(hplo_ok, NX)
                nc.scalar.copy(h_hi[rows(v), v % RING], hf[rows(v), v % 2]).then_inc(hhi_ok, 1)

            def step(i):
                nonlocal u
                kind, h, j = STEPS[i]
                s = slot[i % 2]
                if pending and kind in "trpq":
                    split_h(pending.pop(0))
                if kind in ("t", "u1", "us"):
                    act.wait_ge(z_ok, i + 1)
                if kind == "t":
                    n = t_index(i)
                    cols = slice(h * HALF, (h + 1) * HALF)
                    for k in range(KD):
                        nc.scalar.copy(xt_hi[:, k, cols], s[k][:]).then_inc(thi_ok, 1)
                    if n == 0:
                        split_hi(1)
                elif kind[0] == "u":
                    if u >= 2:
                        act.wait_ge(drained, UNITS[u - 2] + 1)
                    n = P - rows(u).start
                    nc.scalar.activation(sg[rows(u), u % 2], s[0][0:n], ACT.Silu).then_inc(silu_ok, 1)
                    pending.append(u)
                    u += 1
                if len(pending) > 1:
                    split_h(pending.pop(0))
                if i in SPLITS:
                    split_hi(SPLITS[i])
                if i == P_STEP:
                    act.wait_ge(lg_ok, 1)
                    nc.scalar.activation(ee[:], lg[:], ACT.Exp)
                    nc.scalar.activation(top[:], top_lg[:], ACT.Exp)
                    nc.scalar.activation(eg[:], logit[:, :, E2], ACT.Exp, scale=-1.0).then_inc(exp_ok, 1)
                if i == T_STEPS[1]:
                    act.wait_ge(g_in, 16)
                    nc.scalar.copy(g_hi, g_raw[:]).then_inc(ghi_ok, 1)

            for i in range(E_AT):
                step(i)
            for v in pending:
                split_h(v)
            pending.clear()

            def rows_hi(j):
                act.wait_ge(xt_ok, j + 1)
                if j >= 3:
                    act.wait_ge(up_ok, j - 2)
                if j == 2:
                    act.wait_ge(down_ok, LAST_RING + 2)
                nc.scalar.copy(xp_hi[:, ring(j)], slot[j % 2][0][:, 0:D].rearrange("p (k n) -> p k n", k=KD))\
                    .then_inc(xhi_ok, 1)

            def gate_silu(j):
                act.wait_ge(up_ok, j + 1)
                if j >= 2:
                    act.wait_ge(hp_ok, j - 1)
                nc.scalar.activation(sp_[:, j % 2], slot[j % 2][1][:, 0:F2], ACT.Silu).then_inc(sp_ok, 1)

            def hidden_hi(j):
                act.wait_ge(ht_ok, j + 1)
                if j >= 3:
                    act.wait_ge(yd_ok, j - 2)
                nc.scalar.copy(hp_hi[:, ring(j)], slot[j % 2][2][0:NB, 0:D].rearrange("p (b n) -> p b n", b=2))\
                    .then_inc(hphi_ok, 1)

            act.wait_ge(down_ok, LAST_RING + 1)
            rows_hi(0)
            rows_hi(1)
            for j in range(NX + 1):
                if j < NX:
                    gate_silu(j)
                if j + 2 < NX:
                    rows_hi(j + 2)
                if j:
                    hidden_hi(j - 1)
            for i in range(E_AT, len(STEPS)):
                step(i)
            for v in pending:
                split_h(v)
            for t in range(POOL_TILES):
                if t % 2 == 0:
                    act.wait_ge(pair_in[t], 16)
                for k in range(2):
                    row_k = pair_buf(t - t % 2)[:, t % 2, k * D:(k + 1) * D]
                    nc.scalar.activation(row_k, row_k, ACT.Copy, scale=prob[:, t, k:k + 1]).then_inc(scaled, 1)

        @block.vector
        def _(dve):
            links = [0]

            def link(ins):
                links[0] += 1
                ins.then_inc(chain, 1)
                dve.wait_ge(chain, links[0])

            def sums(n, tiles):
                for t in tiles:
                    if n < 2 and t % 2 == 0:
                        dve.wait_ge(x_in[t // 2], 16)
                    last = nc.vector.bn_stats(st[:, t], xs[:, t])
                return last

            def statistics(n, done=0):
                t0 = TH * (n % 2)
                link(sums(n, range(t0 + done, t0 + TH)))
                for t in range(t0, t0 + TH):
                    last = nc.vector.bn_aggr(mv[:, t], st[:, t])
                link(last)
                nc.vector.tensor_scalar(ve[:, t0:t0 + TH], mv[:, t0:t0 + TH, 1], EPS, None,
                                        ALU.add).then_inc(ve_ok, 1)

            def normalize(n):
                dve.wait_ge(rstd_ok, n + 1)
                if n >= 2:
                    dve.wait_ge(z_ok, T_STEPS[n - 2] + 1)
                for t in range(TH * (n % 2), TH * (n % 2) + TH):
                    nc.vector.tensor_scalar(xn[:, t, 0:D], xs[:, t], mv[:, t, 0:1], rstd[:, t:t + 1],
                                            ALU.subtract, ALU.mult).then_inc(xn_ok, 1)

            def masks():
                dve.wait_ge(ids_in, 16)
                link(nc.vector.tensor_scalar(eid[:], idt[:], float(VOCAB // E1), None, ALU.is_ge))
                for k in (2, 3):
                    link(nc.vector.scalar_tensor_tensor(eid[:], idt[:], float(k * (VOCAB // E1)), eid[:],
                                                        ALU.is_ge, ALU.add))
                for e in range(E1):
                    last = nc.vector.tensor_scalar(mask[:, e], eid[:], float(e), None, ALU.is_equal)
                link(last)

            def split_h(v):
                dve.wait_ge(hhi_ok, v + 1)
                if v == NPRE:
                    dve.wait_ge(yd_ok, NX)
                nc.vector.tensor_tensor(h_lo[rows(v), v % RING], hf[rows(v), v % 2],
                                        h_hi[rows(v), v % RING].bitcast(F32), ALU.subtract).then_inc(hlo_ok, 1)

            def choose(h):
                t = slice(h * TH, (h + 1) * TH)
                pairs = [P, TH, E2, E2]
                own = logit[:, t, 0:E2].unsqueeze(3).broadcast_to(pairs)
                other = logit[:, t, 0:E2].unsqueeze(2).broadcast_to(pairs)
                nc.vector.tensor_tensor(larger, other, own, ALU.is_gt)
                link(nc.vector.tensor_tensor(same, other, own, ALU.is_equal))
                link(nc.vector.tensor_tensor(same, same, lower[:].unsqueeze(1).broadcast_to(pairs), ALU.mult))
                link(nc.vector.tensor_tensor(larger, larger, same, ALU.add))
                link(nc.vector.tensor_reduce(rank[:, t], larger, AX.X, ALU.add))
                for k in range(2):
                    last = nc.vector.tensor_scalar(oh[:, k, t], rank[:, t], float(k), None, ALU.is_equal)
                link(last)
                nc.vector.tensor_tensor(chosen[:, t], oh[:, 0, t], oh[:, 1, t], ALU.add).then_inc(chosen_ok, 1)

            def maxima(h):
                for t in range(h * TH, (h + 1) * TH):
                    last = nc.vector.max(m8[:, t], logit[:, t, 0:E2])
                return last

            def tile_experts():
                link(nc.vector.tensor_tensor(past[:], end_t[:].unsqueeze(1).broadcast_to([P, NX, E2]), iota_j[:],
                                             ALU.is_le))
                link(nc.vector.tensor_reduce(te[:], past[:], AX.X, ALU.add))
                link(nc.vector.tensor_scalar(te[:], te[:], float(E2 - 1), None, ALU.min))
                nc.vector.tensor_copy(te_i[:], te[:]).then_inc(tiles_ok, 1)
                dve.wait_ge(tiles_ok, 1)

            def hot_rows(k):
                q = slice(k * NT, (k + 1) * NT)
                nc.vector.tensor_tensor(at_p[:, q], iota_b[:].unsqueeze(1).broadcast_to([P, NT, P]),
                                        place_p[:, q].unsqueeze(2).broadcast_to([P, NT, P]),
                                        ALU.is_equal).then_inc(hot_ok, 1)

            def hot_tiles():
                link(nc.vector.tensor_tensor(at_j[:], iota_j[:, :, 0].unsqueeze(1).broadcast_to([P, 2 * NT, NX]),
                                             place_j[:].unsqueeze(2).broadcast_to([P, 2 * NT, NX]), ALU.is_equal))
                v = val[:].rearrange("p k t v -> p (k t) v")
                for n in range(2):
                    last = nc.vector.tensor_tensor(at_v[:, :, n], at_j[:],
                                                   v[:, :, n:n + 1].broadcast_to([P, 2 * NT, NX]), ALU.mult)
                last.then_inc(hot_ok, 1)

            def exponents():
                link(maxima(1))
                nc.vector.tensor_tensor(top_lg[:], m8[:, :, 0:2], m8[:, :, 0:1].broadcast_to([P, NT, 2]), ALU.subtract)
                nc.vector.tensor_tensor(lg[:], logit[:, :, 0:E2], m8[:, :, 0:1].broadcast_to([P, NT, E2]),
                                        ALU.subtract).then_inc(lg_ok, 1)

            def shared_gate():
                dve.wait_ge(exp_ok, 1)
                link(nc.vector.tensor_scalar(gs[:], eg[:], 1.0, None, ALU.add))
                link(nc.vector.reciprocal(gs[:], gs[:]))

            def probabilities():
                link(nc.vector.tensor_reduce(es[:], ee[:], AX.X, ALU.add))
                link(nc.vector.reciprocal(es[:], es[:]))
                link(nc.vector.tensor_tensor(prob[:], top[:], es[:].unsqueeze(2).broadcast_to([P, NT, 2]), ALU.mult))

            def drain_y(g, h):
                dve.wait_ge(down_ok, GROUP_END[g] + 1)
                if g:
                    dve.wait_ge(y_free, g)
                for t in range(TH):
                    n = h * TH + t
                    y = ybanks[g % 2][t // 2][:, t % 2]
                    weight = mask[:, g % E1, n:n + 1] if g < NG1 else gs[:, n:n + 1]
                    ins = nc.vector.scalar_tensor_tensor(xs[:, n], y, weight, xs[:, n], ALU.mult, ALU.add)
                ins.then_inc(y_free, 1)

            statistics(0)
            sums(1, range(TH, TH + AHEAD))
            normalize(0)
            statistics(1, AHEAD)
            u = 0
            pending = []

            def step(i):
                nonlocal u
                kind, h, j = STEPS[i]
                s = slot[i % 2]
                if pending and kind in "trp":
                    split_h(pending.pop(0))
                dve.wait_ge(z_ok, i + 1)
                if kind == "t":
                    n = t_index(i)
                    cols = slice(h * HALF, (h + 1) * HALF)
                    for k in range(KD):
                        dve.wait_ge(thi_ok, KD * n + k + 1)
                        last = nc.vector.tensor_tensor(xt_lo[:, k, cols], s[k][:],
                                                       xt_hi[:, k, cols].bitcast(F32), ALU.subtract)
                    last.then_inc(drained, 1)
                    if n == 1:
                        masks()
                        dve.wait_ge(ghi_ok, 1)
                        nc.vector.tensor_tensor(g_lo, g_raw[:], g_hi.bitcast(F32),
                                                ALU.subtract).then_inc(g_ok, 1)
                if kind == "r":
                    parts = s[0][:, 0:TH * GW].rearrange("p (t g) -> p t g", g=GW)[:, :, 0:2 * NG]
                    nc.vector.tensor_reduce(logit[:, h * TH:(h + 1) * TH],
                                            parts.rearrange("p t (s g) -> p t g s", s=2), AX.X,
                                            ALU.add).then_inc(drained, 1)
                    dve.wait_ge(drained, i + 1)
                    if h == 1:
                        choose(1)
                elif kind == "p":
                    count = s[1][:, 0:E2]
                    link(nc.vector.tensor_scalar(n_i[:], count, float(P - 1), None, ALU.add))
                    link(nc.vector.tensor_scalar(n_i[:], n_i[:], P.bit_length() - 1, None, ALU.arith_shift_right))
                    link(nc.vector.tensor_copy(n_t[:], n_i[:]))
                    link(nc.vector.tensor_tensor_scan(end_t[:], ones8[:], n_t[:], 0.0, ALU.mult, ALU.add))
                    link(nc.vector.tensor_tensor(start[:], end_t[:], n_t[:], ALU.subtract))
                    link(nc.vector.tensor_scalar(start[:], start[:], float(P), None, ALU.mult))
                    nc.vector.tensor_tensor(place_e[:], s[0][:, 0:NT * E2].rearrange("p (t e) -> p t e", e=E2),
                                            start[:].unsqueeze(1).broadcast_to([P, NT, E2]),
                                            ALU.add).then_inc(drained, 1)
                    dve.wait_ge(drained, i + 1)
                    for k in range(2):
                        last = nc.vector.tensor_tensor(oh[:, k], oh[:, k], place_e[:], ALU.mult)
                    link(last)
                    link(nc.vector.tensor_reduce(place_f[:], oh[:], AX.X, ALU.add))
                    link(nc.vector.tensor_copy(place[:], place_f[:]))
                    link(nc.vector.tensor_scalar(place[:], place[:], P.bit_length() - 1, None, ALU.arith_shift_right))
                    flat = [a[:].rearrange("p k t -> p (k t)") for a in (place, place_f)]
                    link(nc.vector.tensor_copy(place_j[:], flat[0]))
                    link(nc.vector.scalar_tensor_tensor(place_p[:], place_j[:], -float(P), flat[1], ALU.mult, ALU.add))
                elif kind == "q":
                    link(nc.vector.tensor_scalar(row_f[:], s[0][:, 0:NX], -2.0 * P, 2.0 * TOK, ALU.mult, ALU.add))
                    nc.vector.tensor_tensor(row_f[:], row_f[:], s[0][:, NX:2 * NX], ALU.add).then_inc(drained, 1)
                    dve.wait_ge(drained, i + 1)
                    link(nc.vector.tensor_copy(row[:], row_f[:]))
                    nc.vector.tensor_scalar(src[:], row[:], 1, None, ALU.arith_shift_right).then_inc(src_ok, 1)
                elif kind[0] == "u":
                    dve.wait_ge(silu_ok, u + 1)
                    b = s[0] if kind == "u1" or j == NJS - 1 else s[1]
                    if u >= 2:
                        dve.wait_ge(hlo_ok, u - 1)
                    nc.vector.tensor_tensor(hf[rows(u), u % 2], sg[rows(u), u % 2], b[rows(u)],
                                            ALU.mult).then_inc(drained, 1)
                    pending.append(u)
                    u += 1
                if len(pending) > 1 or (pending and kind == "q"):
                    split_h(pending.pop(0))
                if i == P_STEP + 1:
                    hot_rows(0)
                    hot_rows(1)
                    hot_tiles()
                for n in (2, 3):
                    if i == NORM_STEP[n] + 1:
                        normalize(n)
                if i == T_STEPS[0]:
                    normalize(1)
                if i == T_STEPS[3]:
                    choose(0)
                    maxima(0)
                if i == P_STEP - 1:
                    exponents()
                if i == P_STEP + 2:
                    shared_gate()
                if i == Q_STEP:
                    drain_y(NG1, 0)
                    tile_experts()
                if i == Q_STEP + 1:
                    probabilities()
                for g, end in enumerate(GROUP_END):
                    if end in DOWNS[i] and g < NG1:
                        drain_y(g, STEPS[UNITS[end]][1])
                        if g in (E1 - 1, NG1 - 1):
                            dve.wait_ge(y_free, g + 1)
                            statistics(2 + g // E1)

            for i in range(E_AT):
                step(i)
            for v in pending:
                split_h(v)
            pending.clear()

            def rows_lo(j):
                dve.wait_ge(xhi_ok, j + 1)
                nc.vector.tensor_tensor(xp_lo[:, ring(j)], slot[j % 2][0][:, 0:D].rearrange("p (k n) -> p k n", k=KD),
                                        xp_hi[:, ring(j)].bitcast(F32), ALU.subtract).then_inc(xlo_ok, 1)

            def hidden(j):
                dve.wait_ge(sp_ok, j + 1)
                if j >= 2:
                    dve.wait_ge(ht_ok, j - 1)
                nc.vector.tensor_tensor(hp[:, j % 2], sp_[:, j % 2], slot[j % 2][1][:, F2:2 * F2],
                                        ALU.mult).then_inc(hp_ok, 1)

            def hidden_lo(j):
                dve.wait_ge(hphi_ok, j + 1)
                nc.vector.tensor_tensor(hp_lo[:, ring(j)], slot[j % 2][2][0:NB, 0:D].rearrange("p (b n) -> p b n", b=2),
                                        hp_hi[:, ring(j)].bitcast(F32), ALU.subtract).then_inc(hplo_ok, 1)

            def result(j):
                dve.wait_ge(yd_ok, j + 1)
                if j >= 3:
                    dve.wait_ge(back[j % 3], 16 * (j // 3))
                nc.vector.tensor_copy(yp[:, j % 3], yb[j % 2][:, 0]).then_inc(yp_ok, 1)

            rows_lo(0)
            rows_lo(1)
            drain_y(NG1 + 1, 1)
            for j in range(NX + 2):
                if j < NX:
                    hidden(j)
                if j + 2 < NX:
                    rows_lo(j + 2)
                if 1 <= j <= NX:
                    hidden_lo(j - 1)
                if j >= 2:
                    result(j - 2)

            added_n = [0]

            def add_pairs(tiles):
                dve.wait_ge(pair_in[tiles[0] - tiles[0] % 2], 16)
                for k in range(2):
                    for n, t in enumerate(tiles):
                        if k:
                            dve.wait_ge(added, added_n[0] + n + 1)
                        nc.vector.scalar_tensor_tensor(xs[:, t], pair_buf(t - t % 2)[:, t % 2, k * D:(k + 1) * D],
                                                       prob[:, t, k:k + 1], xs[:, t], ALU.mult,
                                                       ALU.add).then_inc(added, 1)
                added_n[0] += 2 * len(tiles)

            for i in range(E_AT, len(STEPS)):
                step(i)
            for v in pending:
                split_h(v)
            for t in range(TH, NT, 2):
                add_pairs([t, t + 1])
            dve.wait_ge(down_ok, len(UNITS))
            dve.wait_ge(added, 2 * TH)
            g = NG1 + 2
            for t in range(TH):
                nc.vector.scalar_tensor_tensor(xs[:, TH + t], ybanks[g % 2][t // 2][:, t % 2], gs[:, TH + t:TH + t + 1],
                                               xs[:, TH + t], ALU.mult, ALU.add).then_inc(out_ok, 1)
            if POOL_TILES < TH:
                add_pairs(range(POOL_TILES, TH))

        @block.tensor
        def _(pe):
            def add(ps, lhs, rhs, start=False, stop=False):
                return nc.tensor.matmul(ps, lhs, rhs, start=start, stop=stop, skip_group_check=True)

            def down(u):
                kind, h, j = STEPS[UNITS[u]]
                pe.wait_ge(hhi_ok, u + 1)
                g = group_of(u)
                if first_of_group(u) and g >= 2:
                    pe.wait_ge(y_free, g - 1)
                if u == NPRE:
                    pe.wait_ge(yp_ok, NX)
                if kind == "u1":
                    w_h, w_l = [a[:, j * P // F1, j % KD, :] for a in (w1_hi, w1_lo)]
                else:
                    w_h, w_l = [a[rows(u), j, 2 * D:3 * D] for a in (ws_hi, ws_lo)]
                tiles = [(ybanks[g % 2][t // 2][:, t % 2], slice(t * P, t * P + P)) for t in range(TH)]
                for t, (y, cols) in enumerate(tiles):
                    add(y, h_hi[rows(u), u % RING, cols], w_h, start=first_of_group(u) and t % 2 == 0)
                    add(y, h_hi[rows(u), u % RING, cols], w_l)
                pe.wait_ge(hlo_ok, u + 1)
                for y, cols in tiles:
                    last = add(y, h_lo[rows(u), u % RING, cols], w_h, stop=ends_group(u))
                last.then_inc(down_ok, 1)

            def rows_t(j):
                pe.wait_ge(rows_ok[j % RX], 16 * (j // RX + 1))
                if j < 2:
                    pe.wait_ge(drained, E_AT - j % 2)
                else:
                    pe.wait_ge(xlo_ok, j - 1)
                for k in range(KD):
                    last = nc.tensor.transpose(slot[j % 2][0][:, k * P:k * P + P],
                                               xr[:, j % RX, k * P:k * P + P], ident[:])
                last.then_inc(xt_ok, 1)

            pe.wait_ge(consts, 2)
            for _ in range(WARM):
                nc.tensor.matmul(slot[1][2][:, 0:P], ones[:], upper[:], start=True, stop=True)
            regs = [pe.alloc_register(f"expert{j}") for j in range(NX)]

            def step(i):
                kind, h, j = STEPS[i]
                s = slot[i % 2]
                if i >= 2:
                    pe.wait_ge(drained, i - 1)
                cols = slice(h * HALF, (h + 1) * HALF)
                if kind == "t":
                    n = t_index(i)
                    pe.wait_ge(xn_ok, TH * (n + 1))
                    for k in range(KD):
                        for t in range(TH):
                            last = nc.tensor.transpose(s[k][:, t * P:t * P + P], xn[:, h * TH + t, k * P:k * P + P],
                                                       ident[:])
                elif kind == "r":
                    pe.wait_ge(drained, T_STEPS[2 + h] + 1)
                    pe.wait_ge(g_ok, 1)
                    for t in range(TH):
                        at = h * HALF + t * P
                        for k in range(KD):
                            nc.tensor.matmul(s[0][:, t * GW:t * GW + 2 * NG], xt_hi[:, k, at:at + P],
                                             g_hl[:, k].rearrange("p s g -> p (s g)"), start=k == 0, stop=False,
                                             skip_group_check=True)
                            last = nc.tensor.matmul(s[0][:, t * GW:t * GW + NG], xt_lo[:, k, at:at + P],
                                                    g_hi[:, k], start=False, stop=k == KD - 1,
                                                    skip_group_check=True)
                elif kind == "p":
                    pe.wait_ge(chosen_ok, 2)
                    flat = chosen[:].rearrange("p t e -> p (t e)")
                    nc.tensor.matmul(s[0][:, 0:NT * E2], upper[:], flat, start=True, stop=False, skip_group_check=True)
                    for d in range(1, NT):
                        nc.tensor.matmul(s[0][:, d * E2:NT * E2], ones[:], flat[:, 0:(NT - d) * E2],
                                         start=False, stop=d == NT - 1, skip_group_check=True)
                    for t in range(NT):
                        last = nc.tensor.matmul(s[1][:, 0:E2], ones[:], chosen[:, t], start=t == 0, stop=t == NT - 1)
                elif kind == "q":
                    pe.wait_ge(hot_ok, 3)
                    for q in range(2 * NT):
                        last = nc.tensor.matmul(s[0][:, 0:2 * NX], at_p[:, q],
                                                at_v[:, q].rearrange("p v j -> p (v j)"),
                                                start=q == 0, stop=q == 2 * NT - 1)
                else:
                    if kind == "u1":
                        n = h
                        split_done(pe, j * P // F1)
                        banks = [[[a[:, j * P // F1, k, (j % 2) * P:(j % 2) * P + P] for a in (w1_hi, w1_lo)]
                                  for k in range(KD)]]
                    else:
                        n = 2 + h
                        split_done(pe, E1 + j)
                        banks = [[[a[:, j, b * D + k * P:b * D + k * P + P] for a in (ws_hi, ws_lo)]
                                  for k in range(KD)] for b in range(2 if j < NJS - 1 else 1)]
                    for b, w in enumerate(banks):
                        for k in range(KD):
                            pe.wait_ge(thi_ok, KD * n + k + 1)
                            add(s[b][:], w[k][0], xt_hi[:, k, cols], start=k == 0)
                            add(s[b][:], w[k][1], xt_hi[:, k, cols])
                        pe.wait_ge(drained, T_STEPS[n] + 1)
                        for k in range(KD):
                            last = add(s[b][:], w[k][0], xt_lo[:, k, cols], stop=k == KD - 1)
                last.then_inc(z_ok, 1)
                if i == E_AT - 1:
                    pe.wait_ge(tiles_ok, 1)
                    nc.tensor.load(regs, te_i[0:1, 0:NX])
                for u in DOWNS[i]:
                    if i == E_AT - 1 and u == LAST_RING + 1:
                        rows_t(0)
                        rows_t(1)
                    down(u)

            def up(j, e):
                pe.wait_ge(xhi_ok, j + 1)
                if j >= 2:
                    pe.wait_ge(hp_ok, j - 1)
                z = slot[j % 2][1][:, 0:2 * F2]
                cols = [bass.ds(e * WX + k * 2 * F2, 2 * F2) for k in range(KD)]
                for k in range(KD):
                    add(z, xp_hi[:, ring(j), k], w_hi[:, cols[k]], start=k == 0)
                    add(z, xp_hi[:, ring(j), k], w_lo[:, cols[k]])
                pe.wait_ge(xlo_ok, j + 1)
                for k in range(KD):
                    last = add(z, xp_lo[:, ring(j), k], w_hi[:, cols[k]], stop=k == KD - 1)
                last.then_inc(up_ok, 1)

            def hidden_t(j):
                pe.wait_ge(hp_ok, j + 1)
                if j >= 2:
                    pe.wait_ge(hplo_ok, j - 1)
                else:
                    pe.wait_ge(y_free, NG1 + 2)
                for b in range(2):
                    last = nc.tensor.transpose(slot[j % 2][2][0:NB, b * P:b * P + P], hp[:, j % 2, b * NB:(b + 1) * NB],
                                               ident[:])
                last.then_inc(ht_ok, 1)

            def down_x(j, e):
                pe.wait_ge(hphi_ok, j + 1)
                if j >= 2:
                    pe.wait_ge(yp_ok, j - 1)
                else:
                    pe.wait_ge(y_free, NG1 + 2)
                y = yb[j % 2][:, 0]
                cols = [bass.ds(e * WX + WU + b * D, D) for b in range(2)]
                for b in range(2):
                    add(y, hp_hi[:, ring(j), b], w_hi[0:NB, cols[b]], start=b == 0)
                    add(y, hp_hi[:, ring(j), b], w_lo[0:NB, cols[b]])
                pe.wait_ge(hplo_ok, j + 1)
                for b in range(2):
                    last = add(y, hp_lo[:, ring(j), b], w_hi[0:NB, cols[b]], stop=b == 1)
                last.then_inc(yd_ok, 1)

            for i in range(E_AT):
                step(i)
            split_done(pe, NSTG - 1)
            expert = {}
            for j in range(NX + 2):
                if j < NX:
                    expert[j] = nc.tensor.snap(regs[j], min_val=0, max_val=E2 - 1)
                    up(j, expert[j])
                if j + 2 < NX:
                    rows_t(j + 2)
                if 1 <= j <= NX:
                    hidden_t(j - 1)
                if j >= 2:
                    down_x(j - 2, expert[j - 2])
            for i in range(E_AT, len(STEPS)):
                step(i)


def kernel(**inputs):
    import numpy as np
    import concourse.bacc as bacc
    from concourse import mybir as mb
    from concourse.bass_utils import run_bass_kernel_spmd

    x = np.ascontiguousarray(inputs["x"]).reshape(TOK, D)
    ids = np.ascontiguousarray(inputs["itok_BxS_13_99985"]).reshape(TOK)
    ctx_t = np.ascontiguousarray(np.asarray(inputs["ctx_2048"]).reshape(E1, F1, KD, P).transpose(3, 0, 2, 1))

    def blocks(a):
        a = a.reshape(*a.shape[:-1], KD, P)
        return np.moveaxis(a, -3, -1).swapaxes(-3, -2)

    ws = np.zeros((NJS, P, WT), np.float32)
    full = NJS - 1
    up = ws[:, :, :2 * D].reshape(NJS, P, 2, KD, P)
    for b, name in enumerate(("shared_fc1", "shared_fc2")):
        w = np.asarray(inputs["L0_ffn_" + name])
        up[:full, :, b] = blocks(w[:full * P].reshape(full, P, D))
        up[full, :, 0, :, b * R:(b + 1) * R] = blocks(w[full * P:])
    ws[:, :, :2 * D] = up.reshape(NJS, P, 2 * D)
    proj = np.asarray(inputs["L0_ffn_shared_proj"]).T
    ws[:full, :, 2 * D:] = proj[:full * P].reshape(full, P, D)
    ws[full, R:, 2 * D:] = proj[full * P:]
    wx = np.zeros((E2, P, WX), np.float32)
    up = wx[:, :, :WU].reshape(E2, P, KD, 2, F2)
    for b, name in enumerate(("expert_fc1", "expert_fc2")):
        up[:, :, :, b] = blocks(np.asarray(inputs["L0_ffn_" + name]))
    wx[:, :, :WU] = up.reshape(E2, P, WU)
    proj = np.asarray(inputs["L0_ffn_expert_proj"]).reshape(E2, D, 2, NB)
    wx[:, :NB, WU:] = proj.transpose(0, 3, 2, 1).reshape(E2, NB, WD)
    gate = np.zeros((P, KD, NG), np.float32)
    gate[:, :, :E2] = np.asarray(inputs["L0_ffn_gate_w"]).reshape(E2, KD, P).transpose(2, 1, 0)
    gate[:, :, E2] = np.asarray(inputs["L0_ffn_shared_gate_w"]).reshape(KD, P).T

    nc = bacc.Bacc("TRN2", target_bir_lowering=False, num_devices=1)
    arrays = {"x_in_dram": x, "ids_dram": ids.reshape(NT, P).T.copy(), "ctx_t_dram": ctx_t, "ws_dram": ws,
              "wx_dram": wx, "gate_dram": gate}
    args = [nc.dram_tensor(k, a.shape, mb.dt.from_np(a.dtype), kind="ExternalInput").ap() for k, a in arrays.items()]
    out = nc.dram_tensor("out_dram", (TOK, D), mb.dt.float32, kind="ExternalOutput").ap()
    program(nc, *args, out)
    r = run_bass_kernel_spmd(nc, [arrays], core_ids=[0])
    return r.results[0]["out_dram"].reshape(inputs["x"].shape)
```
